# Optimizing a Trainium2 kernel written in Bass

```python
import numpy as np
import jax
import jax.numpy as jnp

def _softmax(x, axis=-1):
    return jax.nn.softmax(x, axis=axis)

def _gelu(x):
    return jax.nn.gelu(x, approximate=True)

def _silu(x):
    return jax.nn.silu(x)

def _sigmoid(x):
    return jax.nn.sigmoid(x)

def _layernorm(x, axis=-1, eps=1e-05):
    m = jnp.mean(x, axis=axis, keepdims=True)
    v = jnp.var(x, axis=axis, keepdims=True)
    return (x - m) / jnp.sqrt(v + eps)

def _scatter_add(tgt, idx, src, axis=0):
    return tgt.at[idx].add(src)

def _segment_sum(src, seg, n):
    return jax.ops.segment_sum(src, seg, n)
kernel_name = 'mk_gnn_resnorm_d4_gnn_r8_561e7b'

def setup_inputs(seed: int=0):
    np.random.seed(seed)
    _w = jnp.asarray

    def _rec_inputs():
        import jax
        import jax.numpy as jnp
        _gk = jax.random.key(seed)
        x = -0.0009044 + 1 * jax.random.normal(jax.random.fold_in(_gk, 1), (12500, 16), jnp.float32)
        _s = jax.random.randint(jax.random.fold_in(_gk, 2), (200000,), 0, 12500, jnp.int32)
        _d = jax.random.randint(jax.random.fold_in(_gk, 3), (200000,), 0, 12500, jnp.int32)
        _loop = jnp.arange(12500, dtype=jnp.int32)
        src = jnp.concatenate([_s, _d, _loop])
        dst = jnp.concatenate([_d, _s, _loop])
        _o = jnp.argsort(dst, stable=True)
        src = src[_o]
        dst = dst[_o]
        edge_attr_16 = -0.00010739 + 0.99994 * jax.random.normal(jax.random.fold_in(_gk, 12), (412500, 16), jnp.float32)
        edge_type_8 = jax.random.randint(jax.random.fold_in(_gk, 14), (412500,), 0, 8, jnp.int32)
        return (x, src, dst, edge_attr_16, edge_type_8)
    x, src, dst, edge_attr_16, edge_type_8 = _rec_inputs()

    def _L0_gnn_setup():
        import jax, jax.numpy as jnp
        import numpy as np
        N_NODES = 12500
        N_EDGES = 125000
        MSG_DIM = 16
        HID_DIM = 16
        N_EDGE_TYPE = 8
        key = jax.random.key(seed)
        ks = jax.random.split(key, 9)
        features = jax.random.normal(ks[0], (N_NODES, HID_DIM), dtype=jnp.float32)
        edge_src = jax.random.randint(ks[1], (N_EDGES,), 0, N_NODES, dtype=jnp.int32)
        edge_dst = jax.random.randint(ks[2], (N_EDGES,), 0, N_NODES, dtype=jnp.int32)
        edge_type = jax.random.randint(ks[3], (N_EDGES,), 0, N_EDGE_TYPE, dtype=jnp.int32)
        edge_emb = jax.random.normal(ks[4], (N_EDGE_TYPE, MSG_DIM * HID_DIM), dtype=jnp.float32) * 0.1
        s = 1.0 / np.sqrt(HID_DIM)
        w_ih = jax.random.uniform(ks[5], (3 * HID_DIM, MSG_DIM), minval=-s, maxval=s, dtype=jnp.float32)
        w_hh = jax.random.uniform(ks[6], (3 * HID_DIM, HID_DIM), minval=-s, maxval=s, dtype=jnp.float32)
        b_ih = jax.random.uniform(ks[7], (3 * HID_DIM,), minval=-s, maxval=s, dtype=jnp.float32)
        b_hh = jax.random.uniform(ks[8], (3 * HID_DIM,), minval=-s, maxval=s, dtype=jnp.float32)
        return {'features': features, 'edge_src': edge_src, 'edge_dst': edge_dst, 'edge_type': edge_type, 'edge_emb': edge_emb, 'w_ih': w_ih, 'w_hh': w_hh, 'b_ih': b_ih, 'b_hh': b_hh}
    _L0_gnn_all = _L0_gnn_setup()
    _L0_gnn_in = {k: v for k, v in _L0_gnn_all.items() if k in ('edge_emb', 'w_ih', 'w_hh', 'b_ih', 'b_hh')}
    del _L0_gnn_all

    def _L1_gnn_setup():
        import jax, jax.numpy as jnp
        import numpy as np
        IN_FEATS = 16
        OUT_FEATS = 16
        EDGE_FEATS = 16
        N_NODES = 6250
        N_EDGES = 100000
        key = jax.random.key(seed)
        k = jax.random.split(key, 7)
        feat = jax.random.normal(k[0], (N_NODES, IN_FEATS), dtype=jnp.float32)
        efeat = jax.random.normal(k[1], (N_EDGES, EDGE_FEATS), dtype=jnp.float32)
        We = jax.random.normal(k[2], (EDGE_FEATS, IN_FEATS * OUT_FEATS), dtype=jnp.float32) * 0.1
        be = jax.random.normal(k[3], (IN_FEATS * OUT_FEATS,), dtype=jnp.float32) * 0.1
        bias = jax.random.normal(k[4], (OUT_FEATS,), dtype=jnp.float32) * 0.1
        src = jax.random.randint(k[5], (N_EDGES,), 0, N_NODES, dtype=jnp.int64 if jax.config.jax_enable_x64 else jnp.int32)
        dst = jnp.sort(jax.random.randint(k[6], (N_EDGES,), 0, N_NODES, dtype=jnp.int64 if jax.config.jax_enable_x64 else jnp.int32))
        return {'feat': feat, 'efeat': efeat, 'We': We, 'be': be, 'bias': bias, 'src': src, 'dst': dst, 'num_nodes': N_NODES}
    _L1_gnn_all = _L1_gnn_setup()
    _L1_gnn_in = {k: v for k, v in _L1_gnn_all.items() if k in ('We', 'be', 'bias')}
    del _L1_gnn_all

    def _L2_gnn_setup():
        import jax, jax.numpy as jnp
        import numpy as np
        NUM_ENTITIES = 12500
        NUM_RELATIONS = 8
        NUM_CLASSES = 16
        HIDDEN = 16
        NUM_EDGES = 400000

        def rgcn_conv(x, src, dst, edge_type, W, root, bias):
            num_nodes = x.shape[0]
            x_src = x[src]
            msg = jnp.zeros((src.shape[0], W.shape[2]), x.dtype)
            for r in range(NUM_RELATIONS):
                msg = msg + jnp.where((edge_type == r)[:, None], x_src @ W[r], jnp.zeros((), x.dtype))
            cnt = jnp.zeros((num_nodes, NUM_RELATIONS), x.dtype).at[dst, edge_type].add(1.0)
            norm = 1.0 / jnp.maximum(cnt[dst, edge_type], 1.0)
            agg = jax.ops.segment_sum(msg * norm[:, None], dst, num_segments=num_nodes)
            return agg + x @ root + bias
        key = jax.random.key(seed)
        ks = jax.random.split(key, 9)
        s = 1.0 / np.sqrt(HIDDEN)
        edge_index = jax.random.randint(ks[0], (2, NUM_EDGES), 0, NUM_ENTITIES, dtype=jnp.int32)
        edge_type = jax.random.randint(ks[1], (NUM_EDGES,), 0, NUM_RELATIONS, dtype=jnp.int32)
        return {'embed': jax.random.normal(ks[2], (NUM_ENTITIES, HIDDEN), jnp.float32), 'W1': jax.random.normal(ks[3], (NUM_RELATIONS, HIDDEN, HIDDEN), jnp.float32) * s, 'root1': jax.random.normal(ks[4], (HIDDEN, HIDDEN), jnp.float32) * s, 'b1': jnp.zeros((HIDDEN,), jnp.float32), 'W2': jax.random.normal(ks[5], (NUM_RELATIONS, HIDDEN, NUM_CLASSES), jnp.float32) * s, 'root2': jax.random.normal(ks[6], (HIDDEN, NUM_CLASSES), jnp.float32) * s, 'b2': jnp.zeros((NUM_CLASSES,), jnp.float32), 'edge_index': edge_index, 'edge_type': edge_type}
    _L2_gnn_all = _L2_gnn_setup()
    _L2_gnn_in = {k: v for k, v in _L2_gnn_all.items() if k in ('W1', 'root1', 'b1', 'W2', 'root2', 'b2')}
    del _L2_gnn_all

    def _L3_gnn_setup():
        import jax, jax.numpy as jnp
        import numpy as np
        STALK_DIM = 16
        N_NODES = 6250
        N_EDGES = 50000
        HIDDEN = 64
        key = jax.random.key(seed)
        k1, k2, k3, k4 = jax.random.split(key, 4)
        d = STALK_DIM
        x = jax.random.normal(k1, (N_NODES, d), dtype=jnp.float32)
        edge_index = jax.random.randint(k2, (2, N_EDGES), 0, N_NODES, dtype=jnp.int64)
        W1 = jax.random.normal(k3, (HIDDEN, 2 * d), dtype=jnp.float32) * (1.0 / np.sqrt(2 * d))
        b1 = jnp.zeros((HIDDEN,), dtype=jnp.float32)
        W2 = jax.random.normal(k4, (d, HIDDEN), dtype=jnp.float32) * (1.0 / np.sqrt(HIDDEN))
        b2 = jnp.zeros((d,), dtype=jnp.float32)
        return {'x': x, 'edge_index': edge_index, 'W1': W1, 'b1': b1, 'W2': W2, 'b2': b2}
    _L3_gnn_all = _L3_gnn_setup()
    _L3_gnn_in = {k: v for k, v in _L3_gnn_all.items() if k in ('W1', 'b1', 'W2', 'b2')}
    del _L3_gnn_all
    return {'x': x, 'src': src, 'dst': dst, 'edge_attr_16': edge_attr_16, 'edge_type_8': edge_type_8, 'L0_gnn_edge_emb': _L0_gnn_in['edge_emb'], 'L0_gnn_w_ih': _L0_gnn_in['w_ih'], 'L0_gnn_w_hh': _L0_gnn_in['w_hh'], 'L0_gnn_b_ih': _L0_gnn_in['b_ih'], 'L0_gnn_b_hh': _L0_gnn_in['b_hh'], 'L1_gnn_We': _L1_gnn_in['We'], 'L1_gnn_be': _L1_gnn_in['be'], 'L1_gnn_bias': _L1_gnn_in['bias'], 'L2_gnn_W1': _L2_gnn_in['W1'], 'L2_gnn_root1': _L2_gnn_in['root1'], 'L2_gnn_b1': _L2_gnn_in['b1'], 'L2_gnn_W2': _L2_gnn_in['W2'], 'L2_gnn_root2': _L2_gnn_in['root2'], 'L2_gnn_b2': _L2_gnn_in['b2'], 'L3_gnn_W1': _L3_gnn_in['W1'], 'L3_gnn_b1': _L3_gnn_in['b1'], 'L3_gnn_W2': _L3_gnn_in['W2'], 'L3_gnn_b2': _L3_gnn_in['b2']}

def reference(x, src, dst, edge_attr_16, edge_type_8, L0_gnn_edge_emb, L0_gnn_w_ih, L0_gnn_w_hh, L0_gnn_b_ih, L0_gnn_b_hh, L1_gnn_We, L1_gnn_be, L1_gnn_bias, L2_gnn_W1, L2_gnn_root1, L2_gnn_b1, L2_gnn_W2, L2_gnn_root2, L2_gnn_b2, L3_gnn_W1, L3_gnn_b1, L3_gnn_W2, L3_gnn_b2):
    import jax
    import jax.numpy as jnp

    def _L0_gnn_ref(features, edge_src, edge_dst, edge_type, edge_emb, w_ih, w_hh, b_ih, b_hh):
        import jax, jax.numpy as jnp
        import numpy as np
        N_NODES = 12500
        N_EDGES = 125000
        MSG_DIM = 16
        HID_DIM = 16
        N_EDGE_TYPE = 8
        n_nodes = features.shape[0]
        A = edge_emb[edge_type].reshape(-1, MSG_DIM, HID_DIM)
        h_src = features[edge_src]
        msg = jnp.einsum('emh,eh->em', A, h_src)
        m = jax.ops.segment_sum(msg, edge_dst, num_segments=n_nodes)
        gi = m @ w_ih.T + b_ih
        gh = features @ w_hh.T + b_hh
        i_r, i_z, i_n = jnp.split(gi, 3, axis=-1)
        h_r, h_z, h_n = jnp.split(gh, 3, axis=-1)
        r = jax.nn.sigmoid(i_r + h_r)
        z = jax.nn.sigmoid(i_z + h_z)
        n = jnp.tanh(i_n + r * h_n)
        h_new = (1.0 - z) * n + z * features
        return h_new

    def _L1_gnn_ref(feat, efeat, We, be, bias, src, dst, num_nodes):
        import jax, jax.numpy as jnp
        import numpy as np
        IN_FEATS = 16
        OUT_FEATS = 16
        EDGE_FEATS = 16
        N_NODES = 6250
        N_EDGES = 100000
        w = (efeat @ We + be).reshape(-1, IN_FEATS, OUT_FEATS)
        m = jnp.einsum('ei,eio->eo', feat[src], w)
        neigh = jax.ops.segment_sum(m, dst, num_segments=num_nodes)
        return neigh + feat + bias

    def _L2_gnn_ref(embed, W1, root1, b1, W2, root2, b2, edge_index, edge_type):
        import jax, jax.numpy as jnp
        import numpy as np
        NUM_ENTITIES = 12500
        NUM_RELATIONS = 8
        NUM_CLASSES = 16
        HIDDEN = 16
        NUM_EDGES = 400000

        def rgcn_conv(x, src, dst, edge_type, W, root, bias):
            num_nodes = x.shape[0]
            x_src = x[src]
            msg = jnp.zeros((src.shape[0], W.shape[2]), x.dtype)
            for r in range(NUM_RELATIONS):
                msg = msg + jnp.where((edge_type == r)[:, None], x_src @ W[r], jnp.zeros((), x.dtype))
            cnt = jnp.zeros((num_nodes, NUM_RELATIONS), x.dtype).at[dst, edge_type].add(1.0)
            norm = 1.0 / jnp.maximum(cnt[dst, edge_type], 1.0)
            agg = jax.ops.segment_sum(msg * norm[:, None], dst, num_segments=num_nodes)
            return agg + x @ root + bias
        src, dst = (edge_index[0], edge_index[1])
        h = rgcn_conv(embed, src, dst, edge_type, W1, root1, b1)
        h = jax.nn.relu(h)
        h = rgcn_conv(h, src, dst, edge_type, W2, root2, b2)
        return jax.nn.log_softmax(h, axis=1)

    def _L3_gnn_ref(x, edge_index, W1, b1, W2, b2):
        import jax, jax.numpy as jnp
        import numpy as np
        STALK_DIM = 16
        N_NODES = 6250
        N_EDGES = 50000
        HIDDEN = 64
        d = x.shape[1]
        n = x.shape[0]
        src, dst = (edge_index[0], edge_index[1])
        xs, xd = (x[src], x[dst])

        def reflection(a, b):
            h = jax.nn.relu(jnp.concatenate([a, b], axis=1) @ W1.T + b1)
            return h @ W2.T + b2

        def householder(v):
            vn = v / jnp.maximum(jnp.linalg.norm(v, axis=1, keepdims=True), 1e-12)
            return jnp.eye(d, dtype=v.dtype)[None] - 2.0 * vn[:, :, None] * vn[:, None, :]
        F_s = householder(reflection(xs, xd))
        F_d = householder(reflection(xd, xs))
        L_sd = -jnp.einsum('eki,ekj->eij', F_s, F_d)
        ones_e = jnp.ones(src.shape[0], dtype=x.dtype)
        deg = jnp.zeros(n, dtype=x.dtype).at[src].add(ones_e).at[dst].add(ones_e)
        deg_inv_sqrt = 1.0 / jnp.sqrt(jnp.maximum(deg, 1e-05))
        coef = deg_inv_sqrt[src] * deg_inv_sqrt[dst]
        msg_s = coef[:, None] * jnp.einsum('eij,ej->ei', L_sd, xd)
        msg_d = coef[:, None] * jnp.einsum('eji,ej->ei', L_sd, xs)
        out = x - jnp.zeros_like(x).at[src].add(msg_s) - jnp.zeros_like(x).at[dst].add(msg_d)
        return jax.nn.relu(out)
    edge_index = jnp.stack([src, dst])
    x = _layernorm(x + _L0_gnn_ref(x, src, dst, edge_type_8, L0_gnn_edge_emb, L0_gnn_w_ih, L0_gnn_w_hh, L0_gnn_b_ih, L0_gnn_b_hh), axis=-1)
    x = _layernorm(x + _L1_gnn_ref(x, edge_attr_16, L1_gnn_We, L1_gnn_be, L1_gnn_bias, src, dst, 12500), axis=-1)
    x = _layernorm(x + _L2_gnn_ref(x, L2_gnn_W1, L2_gnn_root1, L2_gnn_b1, L2_gnn_W2, L2_gnn_root2, L2_gnn_b2, edge_index, edge_type_8), axis=-1)
    x = _layernorm(x + _L3_gnn_ref(x, edge_index, L3_gnn_W1, L3_gnn_b1, L3_gnn_W2, L3_gnn_b2), axis=-1)
    return x

_drawn_inputs = setup_inputs


def setup_inputs(seed=0):
    import zlib

    import numpy as np

    out = dict(_drawn_inputs(seed))
    spreads = {'L2_gnn_b1': (0.0, 0.1),
     'L2_gnn_b2': (0.0, 0.1),
     'L3_gnn_b1': (0.0, 0.399),
     'L3_gnn_b2': (0.0, 0.34)}
    factors = {'L1_gnn_bias': 3.838}
    for name, (base, spread) in spreads.items():
        noise = np.random.default_rng([zlib.crc32(name.encode()), seed]).standard_normal(out[name].shape)
        drawn = base * np.exp(spread * noise) if base else spread * noise
        out[name] = jnp.asarray(drawn.astype(out[name].dtype))
    for name, factor in factors.items():
        out[name] = (out[name] * factor).astype(out[name].dtype)
    return out
```

```python
from contextlib import ExitStack, contextmanager

import concourse.bass as bass
import concourse.mybir as mybir
import numpy as np

F32, I32, BF16 = mybir.dt.float32, mybir.dt.int32, mybir.dt.bfloat16
ALU = mybir.AluOpType
ACT = mybir.ActivationFunctionType
AX = mybir.AxisListType

P = 128
N_NODES = 12500
N_EDGES = 412500
D = 16
TYPES = 8
BLOCKS = -(-N_NODES // P)
NODE_PAD = BLOCKS * P
JUNK = NODE_PAD - 1
LAST_NODES = N_NODES - (BLOCKS - 1) * P
REAL_TILES = -(-N_EDGES // P)
LOAD_GROUPS = -(-REAL_TILES // P)
TILES = LOAD_GROUPS * P
LAST_FULL = N_EDGES // P - (LOAD_GROUPS - 1) * P
LAST_EDGES = N_EDGES % P
G = 4
ATTR_TILES = REAL_TILES + 2 * G + 1
T_BIG = 4096.0
ONES = 2
XW = D + ONES
AW = D + 1
X3W = 20
HID = 64
EPS = 1e-5
BOUNDED = "a block's range ends with the last tile, and a step or two of pads follow"


def memory(nc, ctx):
    m = type("Memory", (), {})()
    m.dma_sem = lambda name: ctx.enter_context(nc.semaphore(name))
    sb = lambda name, shape, dt=F32: ctx.enter_context(nc.sbuf_tensor(name, shape, dt))
    m.src_i = sb("src_i", [P, TILES], I32)
    m.dst_f = sb("dst_f", [P, TILES])
    m.type_b = sb("type_b", [P, TILES], BF16)
    m.src_lo = sb("src_lo", [P, TILES], BF16)
    m.src_hi = sb("src_hi", [P, TILES], BF16)
    m.dst_hi = sb("dst_hi", [P, TILES], BF16)
    m.x = sb("x", [P, BLOCKS, XW])
    m.r = sb("r", [P, BLOCKS, 4 * D])
    m.cnt = sb("cnt", [P, BLOCKS, TYPES])
    m.icnt = sb("icnt", [P, BLOCKS, TYPES])
    m.deg = sb("deg", [P, BLOCKS])
    m.x3 = sb("x3", [P, BLOCKS, X3W])
    m.ident = sb("ident", [P, P])
    m.upper = sb("upper", [P, P])
    m.lower = sb("lower", [P, P])
    m.iota = sb("iota", [P, P])
    m.iota_b = sb("iota_b", [P, P], BF16)
    m.iota_blk = sb("iota_blk", [P, BLOCKS])
    m.first = sb("first", [P, BLOCKS])
    m.node = sb("node", [P, BLOCKS])
    m.type_of_col = sb("type_of_col", [P, TYPES * D])
    m.spare_row = sb("spare_row", [P, 1])
    m.zeros = sb("zeros", [P, 384])
    m.steps = sb("steps", [1, BLOCKS + 2], I32)
    m.tile0 = sb("tile0", [1, BLOCKS], I32)
    m.w0a = sb("w0a", [P, 4 * D])
    m.w0x = sb("w0x", [XW, 4 * D])
    m.w1a = sb("w1a", [P, D])
    m.w1b = sb("w1b", [P, D])
    m.w1c = sb("w1c", [D, D])
    m.bias1 = sb("bias1", [P, D])
    m.w2a = sb("w2a", [P, 2, D])
    m.w2x = sb("w2x", [XW, 2, D])
    m.w3n = sb("w3n", [XW, 2 * HID])
    m.w3e = sb("w3e", [D, 2 * HID])
    m.w3v = sb("w3v", [2 * HID, 2 * D])
    m.bias3 = sb("bias3", [P, 2 * D])
    return m


@contextmanager
def stage_semaphores(nc, prefix):
    with ExitStack() as ctx:
        used = []

        def sem(name):
            used.append(ctx.enter_context(nc.semaphore(f"{prefix}_{name}")))
            return used[-1]

        yield sem
        with nc.Block() as block:
            @block.sync
            def _(sp):
                for s in used:
                    sp.sem_clear(s)


def load_and_constants(nc, m, a, tables):
    with ExitStack() as ctx:
        sb = lambda name, shape, dt=F32: ctx.enter_context(nc.sbuf_tensor(name, shape, dt))
        pb = lambda name, shape: ctx.enter_context(nc.psum_tensor(name, shape, F32))
        sem = ctx.enter_context(stage_semaphores(nc, "load"))
        raw = [sb(f"raw{n}", [P, LOAD_GROUPS, P], I32) for n in range(3)]
        row = [sb(f"row{n}", [P, P]) for n in range(3)]
        wih = sb("wih", [D, 3 * D])
        emb = sb("emb", [D, TYPES * D])
        hist_hi = sb("hist_hi", [P, TILES], I32)
        tmin = sb("tmin", [P, LOAD_GROUPS])
        tmax = sb("tmax", [P, LOAD_GROUPS])
        tnum = sb("tnum", [P, LOAD_GROUPS])
        tback = sb("tback", [P, LOAD_GROUPS])
        has = sb("has", [P, BLOCKS, LOAD_GROUPS])
        has2 = sb("has2", [P, BLOCKS, LOAD_GROUPS])
        ends = sb("ends", [P, 2, BLOCKS])
        span = sb("span", [BLOCKS, 6])
        span_i = sb("span_i", [BLOCKS, 2], I32)
        odd = sb("odd", [1, 2], I32)
        ps_w = pb("ps_w", [P, 3 * D])
        ps_t = [pb(f"ps_t{n}", [P, P]) for n in range(3)]
        ps_e = pb("ps_e", [P, 2, P])
        ps_s = pb("ps_s", [1, 2, P])

        ids_in, x_in, w_in, x_out = (m.dma_sem(n) for n in ("ids_in", "x_in", "w_in", "x_out"))
        ids_filled, x_zeroed = sem("ids_filled"), sem("x_zeroed")
        consts_made, zeros_made = sem("consts_made"), sem("zeros_made")
        masks_zeroed = sem("masks_zeroed")
        rows_ready, cols_in_psum, cols_taken, w0_in_psum, ends_ready, ends_in_psum, span_ready, span_in_psum = (
            sem(n) for n in ("rows_ready", "cols_in_psum", "cols_taken", "w0_in_psum", "ends_ready", "ends_in_psum",
                             "span_ready", "span_in_psum"))
        dve_step = sem("dve_step0")
        n_w = [0]

        with nc.Block() as block:
            @block.sync
            def _(sp):
                ids = (a["src"], a["dst"], a["edge_type_8"])
                full = (LOAD_GROUPS - 1) * P * P
                for n in range(3):
                    sp.dma_start(raw[n][:, 0:LOAD_GROUPS - 1, :],
                                 ids[n][0:full].rearrange("(j t e) -> t j e", t=P, e=P)).then_inc(ids_in, 16)
                sp.wait_ge(ids_filled, 3)
                for n in range(3):
                    sp.dma_start(raw[n][0:LAST_FULL, LOAD_GROUPS - 1, :],
                                 ids[n][full:full + LAST_FULL * P].rearrange("(t e) -> t e", e=P)).then_inc(ids_in, 16)
                    sp.dma_start(raw[n][LAST_FULL:LAST_FULL + 1, LOAD_GROUPS - 1, 0:LAST_EDGES],
                                 ids[n][full + LAST_FULL * P:N_EDGES].rearrange("(t e) -> t e", t=1)).then_inc(ids_in, 16)
                sp.wait_ge(x_zeroed, 2)
                whole = (BLOCKS - 1) * P
                sp.dma_start(m.x[:, 0:BLOCKS - 1, 0:D],
                             a["x"][0:whole, :].rearrange("(b p) f -> p b f", p=P)).then_inc(x_in, 16)
                sp.dma_start(m.x[0:LAST_NODES, BLOCKS - 1, 0:D], a["x"][whole:N_NODES, :]).then_inc(x_in, 16)
                sp.wait_ge(x_in, 32)
                sp.dma_start(tables[0].rearrange("(b p) f -> p b f", p=P), m.x[:, :, 0:D]).then_inc(x_out, 16)
                sp.wait_ge(x_out, 16)

            def small_loads():
                row1 = lambda v: v.rearrange("(a j) -> a j", a=1)
                yield wih[:, :], a["w_ih_t"]
                yield emb[:, :], a["emb_t"]
                yield m.w0x[0:D, 0:2 * D], a["w_hh_t"][:, 0:2 * D]
                yield m.w0x[0:D, 3 * D:4 * D], a["w_hh_t"][:, 2 * D:3 * D]
                yield m.w0x[D:D + 1, 0:3 * D], row1(a["L0_gnn_b_ih"])
                yield m.w0x[D + 1:D + 2, 0:2 * D], row1(a["L0_gnn_b_hh"][0:2 * D])
                yield m.w0x[D + 1:D + 2, 3 * D:4 * D], row1(a["L0_gnn_b_hh"][2 * D:3 * D])
                we = a["L1_gnn_We"].rearrange("f (i o) -> (f i) o", o=D)
                yield m.w1a[:, :], we[0:P, :]
                yield m.w1b[:, :], we[P:2 * P, :]
                yield m.w1c[:, :], a["L1_gnn_be"].rearrange("(i o) -> i o", o=D)
                yield m.bias1[:, :], a["L1_gnn_bias"].partition_broadcast(P)
                for layer, (w, root, b) in enumerate((("L2_gnn_W1", "L2_gnn_root1", "L2_gnn_b1"),
                                                      ("L2_gnn_W2", "L2_gnn_root2", "L2_gnn_b2"))):
                    yield m.w2a[:, layer, :], a[w].rearrange("t f o -> (t f) o")
                    yield m.w2x[0:D, layer, :], a[root]
                    yield m.w2x[D:D + 1, layer, :], row1(a[b])
                yield m.w3n[0:D, 0:HID], a["w3_1_t"][D:2 * D, :]
                yield m.w3n[0:D, HID:2 * HID], a["w3_1_t"][0:D, :]
                yield m.w3n[D:D + 1, 0:HID], row1(a["L3_gnn_b1"])
                yield m.w3n[D:D + 1, HID:2 * HID], row1(a["L3_gnn_b1"])
                yield m.w3e[:, 0:HID], a["w3_1_t"][0:D, :]
                yield m.w3e[:, HID:2 * HID], a["w3_1_t"][D:2 * D, :]
                yield m.w3v[0:HID, 0:D], a["w3_2_t"]
                yield m.w3v[HID:2 * HID, D:2 * D], a["w3_2_t"]
                for n in range(2):
                    yield m.bias3[:, n * D:(n + 1) * D], a["L3_gnn_b2"].partition_broadcast(P)

            n_w[0] = len(list(small_loads()))

            @block.scalar
            def _(act):
                act.wait_ge(zeros_made, 4)
                for out, in_ in small_loads():
                    act.dma_start(out, in_).then_inc(w_in, 16)

                def group(j):
                    act.wait_ge(cols_in_psum, j + 1)
                    nc.scalar.copy(m.src_i[:, bass.ds(j * P, P)], ps_t[0][:, :])
                    nc.scalar.copy(m.dst_f[:, bass.ds(j * P, P)], ps_t[1][:, :])
                    nc.scalar.copy(m.type_b[:, bass.ds(j * P, P)], ps_t[2][:, :]).then_inc(cols_taken, 1)

                with act.Fori(0, LOAD_GROUPS) as j:
                    group(j)
                act.wait_ge(w_in, 16 * n_w[0])

            @block.gpsimd
            def _(pool):
                g = nc.gpsimd
                small = dict(allow_small_or_imprecise_dtypes=True)
                g.memset(m.ident[:, :], 0.0).then_inc(masks_zeroed, 1)
                g.memset(m.upper[:, :], 1.0).then_inc(masks_zeroed, 1)
                g.memset(m.lower[:, :], 1.0).then_inc(masks_zeroed, 1)
                pool.wait_ge(masks_zeroed, 3)
                g.affine_select(out=m.ident[:, :], in_=m.ident[:, :], compare_op=ALU.not_equal, fill=1.0, base=0,
                                pattern=[[-1, P]], channel_multiplier=1).then_inc(consts_made, 1)
                g.affine_select(out=m.upper[:, :], in_=m.upper[:, :], compare_op=ALU.is_gt, fill=0.0, base=0,
                                pattern=[[1, P]], channel_multiplier=-1).then_inc(consts_made, 1)
                g.affine_select(out=m.lower[:, :], in_=m.lower[:, :], compare_op=ALU.is_gt, fill=0.0, base=0,
                                pattern=[[-1, P]], channel_multiplier=1).then_inc(consts_made, 1)
                g.iota(m.iota[:, :], [[1, P]], base=0, channel_multiplier=0, **small)
                g.iota(m.iota_b[:, :], [[1, P]], base=0, channel_multiplier=0, **small)
                g.iota(m.iota_blk[:, :], [[1, BLOCKS]], base=0, channel_multiplier=0, **small)
                g.iota(m.first[:, :], [[P, BLOCKS]], base=0, channel_multiplier=0, **small)
                g.iota(m.node[:, :], [[P, BLOCKS]], base=0, channel_multiplier=1, **small)
                g.iota(m.type_of_col[:, :], [[1, TYPES], [0, D]], base=0, channel_multiplier=0, **small)
                g.iota(m.spare_row[:, :], [[0, 1]], base=NODE_PAD, channel_multiplier=1, **small)
                g.iota(tnum[:, :], [[P, LOAD_GROUPS]], base=1, channel_multiplier=1, **small)
                g.iota(tback[:, :], [[-P, LOAD_GROUPS]], base=int(T_BIG), channel_multiplier=-1, **small)\
                    .then_inc(consts_made, 1)

            @block.tensor
            def _(pe):
                pe.wait_ge(consts_made, 4)
                with pe.Fori(0, LOAD_GROUPS) as j:
                    pe.wait_ge(rows_ready, j + 1)
                    pe.wait_ge(cols_taken, j)
                    for n in range(3):
                        last = nc.tensor.transpose(ps_t[n][:, :], row[n][:, :], m.ident[:, :])
                    last.then_inc(cols_in_psum, 1)
                pe.wait_ge(w_in, 16 * n_w[0])
                nc.tensor.matmul(ps_w[:, :], emb[:, :], wih[:, :], start=True, stop=True).then_inc(w0_in_psum, 1)
                pe.wait_ge(ends_ready, 1)
                nc.tensor.transpose(ps_e[0:BLOCKS, 0, :], ends[:, 0, :], m.ident[:, :])
                nc.tensor.transpose(ps_e[0:BLOCKS, 1, :], ends[:, 1, :], m.ident[:, :]).then_inc(ends_in_psum, 1)
                pe.wait_ge(span_ready, 1)
                nc.tensor.matmul(ps_s[0:1, 0, 0:BLOCKS + 1], span[:, 4:5], m.upper[0:BLOCKS, 0:BLOCKS + 1],
                                 start=True, stop=True)
                nc.tensor.matmul(ps_s[0:1, 1, 0:BLOCKS], span[:, 2:3], m.ident[0:BLOCKS, 0:BLOCKS],
                                 start=True, stop=True).then_inc(span_in_psum, 1)

            @block.vector
            def _(dve):
                v = nc.vector
                count = [0]

                def link(ins):
                    count[0] += 1
                    ins.then_inc(dve_step, 1)
                    dve.wait_ge(dve_step, count[0])

                for n, pad in enumerate((JUNK, JUNK, 0)):
                    v.memset(raw[n][:, LOAD_GROUPS - 1, :], pad).then_inc(ids_filled, 1)
                v.memset(m.x[:, :, D:XW], 1.0).then_inc(x_zeroed, 1)
                v.memset(m.x[:, BLOCKS - 1, 0:D], 0.0).then_inc(x_zeroed, 1)
                v.memset(m.w0x[:, :], 0.0).then_inc(zeros_made, 1)
                v.memset(m.w2x[:, :, :], 0.0).then_inc(zeros_made, 1)
                v.memset(m.w3n[:, :], 0.0).then_inc(zeros_made, 1)
                v.memset(m.w3v[:, :], 0.0).then_inc(zeros_made, 1)
                v.memset(m.zeros[:, :], 0.0)
                v.memset(m.x3[:, :, :], 0.0)
                v.memset(m.w0a[:, :], 0.0)
                dve.wait_ge(ids_in, 16 * 9)
                with dve.Fori(0, LOAD_GROUPS) as j:
                    dve.wait_ge(cols_in_psum, j)
                    for n in range(3):
                        last = v.tensor_copy(row[n][:, :], raw[n][:, bass.ds(j, 1), :])
                    last.then_inc(rows_ready, 1)
                v.tensor_reduce(tmin[:, :], raw[1][:, :, :], AX.X, ALU.min)
                link(v.tensor_reduce(tmax[:, :], raw[1][:, :, :], AX.X, ALU.max))
                dve.wait_ge(consts_made, 4)
                wide = [P, BLOCKS, LOAD_GROUPS]
                per_tile = lambda t: t[:, :].unsqueeze(1).to_broadcast(wide)
                per_block = lambda t: t[:, :].unsqueeze(2).to_broadcast(wide)
                link(v.tensor_scalar(tmin[:, :], tmin[:, :], float(P), None, ALU.subtract))
                v.tensor_tensor(has[:, :, :], per_tile(tmin), per_block(m.first), ALU.is_lt)
                link(v.tensor_tensor(has2[:, :, :], per_tile(tmax), per_block(m.first), ALU.is_ge))
                link(v.tensor_tensor(has[:, :, :], has[:, :, :], has2[:, :, :], ALU.mult))
                link(v.tensor_tensor(has2[:, :, :], has[:, :, :], per_tile(tnum), ALU.mult))
                link(v.tensor_reduce(ends[:, 0, :], has2[:, :, :], AX.X, ALU.max))
                link(v.tensor_tensor(has2[:, :, :], has[:, :, :], per_tile(tback), ALU.mult))
                v.tensor_reduce(ends[:, 1, :], has2[:, :, :], AX.X, ALU.max).then_inc(ends_ready, 1)
                dve.wait_ge(w0_in_psum, 1)
                v.tensor_copy(m.w0a[:, 0:3 * D], ps_w[:, :])
                dve.wait_ge(ends_in_psum, 1)
                link(v.tensor_reduce(span[:, 0:2], ps_e[0:BLOCKS, :, :], AX.X, ALU.max))
                link(v.tensor_scalar(span[:, 2:3], span[:, 1:2], -1.0, T_BIG, ALU.mult, ALU.add))
                link(v.tensor_scalar(span[:, 2:3], span[:, 2:3], float(REAL_TILES - 1), None, ALU.min))
                link(v.tensor_scalar(span[:, 0:1], span[:, 0:1], float(REAL_TILES), None, ALU.min))
                link(v.tensor_tensor(span[:, 3:4], span[:, 0:1], span[:, 2:3], ALU.subtract))
                link(v.tensor_scalar(span_i[:, 0:1], span[:, 3:4], float(G - 1), 1.0, ALU.add, ALU.max))
                link(v.tensor_scalar(span_i[:, 1:2], span_i[:, 0:1], G.bit_length() - 1, None, ALU.arith_shift_right))
                v.tensor_scalar(span[:, 4:5], span_i[:, 1:2], 1.0, None, ALU.max).then_inc(span_ready, 1)
                dve.wait_ge(span_in_psum, 1)
                v.tensor_copy(m.tile0[:, :], ps_s[0:1, 1, 0:BLOCKS])
                link(v.tensor_copy(m.steps[0:1, 0:BLOCKS + 1], ps_s[0:1, 0, 0:BLOCKS + 1]))
                link(v.tensor_scalar(odd[:, 0:1], m.steps[0:1, BLOCKS:BLOCKS + 1], 1, None, ALU.bitwise_and))
                link(v.tensor_tensor(m.steps[0:1, BLOCKS:BLOCKS + 1], m.steps[0:1, BLOCKS:BLOCKS + 1], odd[:, 0:1],
                                     ALU.add))
                v.tensor_scalar(m.steps[0:1, BLOCKS + 1:BLOCKS + 2], m.steps[0:1, BLOCKS:BLOCKS + 1], 2.0, None,
                                ALU.subtract)
                dve.wait_ge(cols_taken, LOAD_GROUPS)
                link(v.tensor_scalar(hist_hi[:, :], m.src_i[:, :], P - 1, None, ALU.bitwise_and))
                link(v.tensor_copy(m.src_lo[:, :], hist_hi[:, :]))
                link(v.tensor_scalar(hist_hi[:, :], m.src_i[:, :], 7, None, ALU.logical_shift_right))
                link(v.tensor_copy(m.src_hi[:, :], hist_hi[:, :]))
                link(v.tensor_copy(hist_hi[:, :], m.dst_f[:, :]))
                link(v.tensor_scalar(hist_hi[:, :], hist_hi[:, :], 7, None, ALU.logical_shift_right))
                v.tensor_copy(m.dst_hi[:, :], hist_hi[:, :])


def edge_pass(nc, m, name, table, by_attr=None, count=False, by_count=None, out_degree=False, weights=(), width=D):
    wide = AW if by_attr is not None else TYPES
    cols = wide * D
    with ExitStack() as ctx:
        sb = lambda n, shape, dt=F32: ctx.enter_context(nc.sbuf_tensor(f"{name}_{n}", shape, dt))
        pb = lambda n, shape: ctx.enter_context(nc.psum_tensor(f"{name}_{n}", shape, F32))
        sem = ctx.enter_context(stage_semaphores(nc, name))
        idx = sb("idx", [P, G], I32)
        xg = sb("xg", [P, G, D])
        sel = sb("sel", [P, G, P])
        outer = sb("outer", [P, G, cols + TYPES])
        attr = sb("attr", [P, G, AW]) if by_attr is not None else None
        node_row = sb("node_row", [P, P])
        own = sb("own", [P, cols + XW])
        own_t = sb("own_t", [P, 3, P])
        mask = sb("mask", [P, G], BF16)
        lo1 = sb("lo1", [P, G, P], BF16)
        hi1 = sb("hi1", [P, G, BLOCKS], BF16)
        zb = sb("zb", [P, P], BF16)
        acc = pb("acc", [P, cols + (TYPES if count else 0)])
        acc_t = pb("acc_t", [P, 3, P])
        res = pb("res", [P, width])
        hist = pb("hist", [P, BLOCKS])
        chunks = []
        for c in range(0, cols, P):
            chunks.append((c, min(P, cols - c)))
        if by_attr is None:
            chunks.append((cols, XW))
        assert len(chunks) == len(weights)

        idx_ready, used, summed, ready = sem("idx_ready"), sem("used"), sem("summed"), sem("ready")
        landed = [m.dma_sem(f"{name}_landed{k}") for k in range(G)]
        attr_in = [m.dma_sem(f"{name}_attr_in{k}") for k in range(G)] if by_attr is not None else []
        row_made, block_summed, own_made, own_turned, turned_out, multiplied, stored = (
            sem(n) for n in ("row_made", "block_summed", "own_made", "own_turned", "turned_out", "multiplied", "stored"))
        masked, ones_made, passed, sp_passed = sem("masked"), sem("ones_made"), sem("passed"), sem("sp_passed")

        def block_range(eng, b):
            i0 = eng.value_load(m.steps[0:1, bass.ds(b, 1)], min_val=0, max_val=1 << 20)
            i1 = eng.value_load(m.steps[0:1, bass.ds(b + 1, 1)], min_val=1, max_val=1 << 20)
            return i0, i1

        def first_tile(eng, b):
            return eng.value_load(m.tile0[0:1, bass.ds(b, 1)], min_val=0, max_val=REAL_TILES - 1)

        def tile(t0, i, i0, k=0, n=1):
            at = nc.s_assert_within(t0 + (i - i0) * G + k, 0, TILES - n, skip_runtime_bounds_check_because=BOUNDED)
            return bass.ds(at, n)

        with nc.Block() as block:
            @block.scalar
            def _(act):
                with act.Fori(0, BLOCKS) as b:
                    i0, i1 = block_range(act, b)
                    t0 = first_tile(act, b)
                    with act.Fori(i0, i1) as i:
                        for k in range(G):
                            act.wait_ge(used, i * G + k + 1)
                            nc.scalar.copy(idx[:, k:k + 1], m.src_i[:, tile(t0, i, i0, k)]).then_inc(idx_ready, 1)

            @block.gpsimd
            def _(pool):
                n_steps = pool.value_load(m.steps[0:1, BLOCKS:BLOCKS + 1], min_val=1, max_val=1 << 20)
                with pool.Fori(0, n_steps) as i:
                    for k in range(G):
                        pool.wait_ge(idx_ready, i * G + k + 1)
                        pool.sem_inc(passed, 1)
                        nc.gpsimd.indirect_dma_start(
                            out=xg[:, k, :], out_offset=None, in_=table,
                            in_offset=bass.IndirectOffsetOnAxis(ap=idx[:, k:k + 1], axis=0)).then_inc(landed[k], 16)

            if by_attr is not None:
                @block.sync
                def _(sp):
                    rows = by_attr.rearrange("(t p) f -> p t f", p=P)
                    with sp.Fori(0, BLOCKS) as b:
                        i0, i1 = block_range(sp, b)
                        t0 = first_tile(sp, b)
                        with sp.Fori(i0, i1) as i:
                            for k in range(G):
                                at = nc.s_assert_within(t0 + (i - i0) * G + k, 0, ATTR_TILES - 1, skip_runtime_bounds_check_because=BOUNDED)
                                sp.wait_ge(used, i * G + k + 1)
                                sp.sem_inc(sp_passed, 1)
                                sp.dma_start(attr[:, k:k + 1, 0:D], rows[:, bass.ds(at, 1), :]).then_inc(attr_in[k], 16)

            @block.tensor
            def _(pe):
                if out_degree:
                    pe.wait_ge(ones_made, 1)
                    nc.tensor.matmul(hist[:, :], zb[:, :], zb[:, 0:BLOCKS], start=True, stop=False, skip_group_check=True)
                with pe.Fori(0, BLOCKS) as b:
                    i0, i1 = block_range(pe, b)
                    zero = m.zeros[:, 0:acc.shape[1]]
                    nc.tensor.matmul(acc[:, :], m.zeros[:, 0:P], zero, start=True, stop=False, skip_group_check=True)
                    with pe.Fori(i0, i1) as i:
                        for k in range(G):
                            pe.wait_ge(used, i * G + k + 1 + G)
                            if out_degree:
                                nc.tensor.matmul(hist[:, :], lo1[:, k, :], hi1[:, k, :], start=False, stop=False,
                                                 skip_group_check=True)
                            nc.tensor.matmul(acc[:, :], sel[:, k, :], outer[:, k, 0:acc.shape[1]], start=False,
                                             stop=False, skip_group_check=True).then_inc(summed, 1)
                    nc.tensor.matmul(acc[:, :], m.zeros[:, 0:P], zero, start=False, stop=True,
                                     skip_group_check=True).then_inc(block_summed, 1)
                    pe.wait_ge(own_made, b + 1)
                    for n, (c, w) in enumerate(chunks):
                        last = nc.tensor.transpose(acc_t[0:w, n, :], own[:, c:c + w], m.ident[:, :])
                    last.then_inc(own_turned, 1)
                    pe.wait_ge(turned_out, b + 1)
                    for n, (c, w) in enumerate(chunks):
                        last = nc.tensor.matmul(res[:, :], own_t[0:w, n, :], weights[n], start=n == 0,
                                                stop=n == len(chunks) - 1)
                    last.then_inc(multiplied, 1)
                if out_degree:
                    nc.tensor.matmul(hist[:, :], zb[:, :], zb[:, 0:BLOCKS], start=False, stop=True,
                                     skip_group_check=True).then_inc(multiplied, 1)

            @block.vector
            def _(dve):
                v = nc.vector
                if attr is not None:
                    v.memset(attr[:, :, D:AW], 1.0).then_inc(ones_made, 1)
                    dve.wait_ge(ones_made, 1)
                if out_degree:
                    v.memset(zb[:, :], 0.0).then_inc(ones_made, 1)
                dve.sem_inc(used, G)
                dve.sem_inc(summed, G)
                with dve.Fori(0, BLOCKS) as b:
                    i0, i1 = block_range(dve, b)
                    t0 = first_tile(dve, b)
                    v.tensor_scalar(node_row[:, :], m.iota[:, :], m.first[:, bass.ds(b, 1)], None,
                                    ALU.add).then_inc(row_made, 1)
                    with dve.Fori(i0, i1) as i:
                        dve.wait_ge(row_made, b + 1)
                        if out_degree:
                            dve.wait_ge(summed, (i + 1) * G)
                            v.tensor_scalar(mask[:, :], m.dst_hi[:, tile(t0, i, i0, 0, G)], m.iota_blk[:, bass.ds(b, 1)],
                                            None, ALU.is_equal).then_inc(masked, 1)
                            dve.wait_ge(masked, i + 1)
                        for k in range(G):
                            dve.wait_ge(summed, i * G + k + 1)
                            v.tensor_scalar(sel[:, k, :], node_row[:, :], m.dst_f[:, tile(t0, i, i0, k)], None, ALU.is_equal)
                            if out_degree:
                                v.tensor_scalar(lo1[:, k, :], m.iota_b[:, :], m.src_lo[:, tile(t0, i, i0, k)],
                                                mask[:, k:k + 1], ALU.is_equal, ALU.mult)
                                v.tensor_scalar(hi1[:, k, :], m.iota_b[:, 0:BLOCKS], m.src_hi[:, tile(t0, i, i0, k)],
                                                None, ALU.is_equal)
                            if count:
                                v.tensor_scalar(outer[:, k, cols:cols + TYPES], m.iota[:, 0:TYPES],
                                                m.type_b[:, tile(t0, i, i0, k)], None, ALU.is_equal)
                            out = outer[:, k, 0:cols].rearrange("p (w f) -> p w f", f=D)
                            feats = xg[:, k, :].unsqueeze(1).to_broadcast([P, wide, D])
                            dve.wait_ge(landed[k], (i + 1) * 16)
                            if attr is not None:
                                dve.wait_ge(attr_in[k], (i + 1) * 16)
                                v.tensor_tensor(out, attr[:, k, :].unsqueeze(2).to_broadcast([P, wide, D]), feats,
                                                ALU.mult).then_inc(used, 1)
                            else:
                                kinds = m.type_of_col[:, :].rearrange("p (w f) -> p w f", f=D)
                                v.scalar_tensor_tensor(out, kinds, m.type_b[:, tile(t0, i, i0, k)], feats,
                                                       ALU.is_equal, ALU.mult).then_inc(used, 1)
                    dve.wait_ge(block_summed, b + 1)
                    at = bass.ds(b, 1)
                    if by_count is not None:
                        v.tensor_tensor(own[:, 0:cols].rearrange("p (w f) -> p w f", f=D),
                                        acc[:, 0:cols].rearrange("p (w f) -> p w f", f=D),
                                        by_count[:, at, :].squeeze(1).unsqueeze(2).to_broadcast([P, TYPES, D]), ALU.mult)
                    else:
                        v.tensor_copy(own[:, 0:cols], acc[:, 0:cols])
                    if count:
                        v.tensor_copy(m.cnt[:, at, :].squeeze(1), acc[:, cols:cols + TYPES])
                    v.tensor_copy(own[:, cols:cols + XW], m.x[:, at, :].squeeze(1)).then_inc(own_made, 1)
                    dve.wait_ge(own_turned, b + 1)
                    for n, (c, w) in enumerate(chunks):
                        last = v.tensor_copy(own_t[0:w, n, :], acc_t[0:w, n, :])
                    last.then_inc(turned_out, 1)
                    dve.wait_ge(multiplied, b + 1)
                    v.tensor_copy(m.r[:, at, 0:width].squeeze(1), res[:, :])
                if out_degree:
                    dve.wait_ge(multiplied, BLOCKS + 1)
                    v.tensor_copy(m.deg[:, :], hist[:, :])


def node_pass(nc, m, name, body, table_out=None):
    with ExitStack() as ctx:
        sb = lambda n, shape, dt=F32: ctx.enter_context(nc.sbuf_tensor(f"{name}_{n}", shape, dt))
        sem = ctx.enter_context(stage_semaphores(nc, name))
        tmp = [sb(f"tmp{n}", [P, BLOCKS, D]) for n in range(4)]
        one = [sb(f"one{n}", [P, BLOCKS]) for n in range(2)]
        step, to_act, from_act, x_ready = (sem(n) for n in ("step", "to_act", "from_act", "x_ready"))
        x_out = m.dma_sem(f"{name}_x_out")
        asked = []

        with nc.Block() as block:
            @block.vector
            def _(dve):
                v = nc.vector
                count = [0]

                def link(ins):
                    count[0] += 1
                    ins.then_inc(step, 1)
                    dve.wait_ge(step, count[0])

                def on_act(ins, func, out, in_):
                    ins.then_inc(to_act, 1)
                    asked.append((func, out, in_))
                    dve.wait_ge(from_act, len(asked))

                per_node = lambda t: t[:, :].unsqueeze(2).to_broadcast([P, BLOCKS, D])
                body(v, link, on_act, tmp, one, per_node)
                y, z = tmp[0][:, :, :], tmp[1][:, :, :]
                out = m.x[:, :, 0:D]
                link(v.tensor_reduce(one[0][:, :], y, AX.X, ALU.add))
                link(v.tensor_scalar(one[0][:, :], one[0][:, :], 1.0 / D, None, ALU.mult))
                link(v.tensor_tensor(y, y, per_node(one[0]), ALU.subtract))
                link(v.tensor_tensor(z, y, y, ALU.mult))
                link(v.tensor_reduce(one[0][:, :], z, AX.X, ALU.add))
                on_act(v.tensor_scalar(one[0][:, :], one[0][:, :], 1.0 / D, EPS, ALU.mult, ALU.add),
                       ACT.Sqrt, one[1][:, :], one[0][:, :])
                link(v.reciprocal(one[1][:, :], one[1][:, :]))
                v.tensor_tensor(out, y, per_node(one[1]), ALU.mult).then_inc(x_ready, 1)

            @block.scalar
            def _(act):
                for n, (func, out, in_) in enumerate(asked):
                    act.wait_ge(to_act, n + 1)
                    nc.scalar.activation(out, in_, func).then_inc(from_act, 1)

            @block.sync
            def _(sp):
                if table_out is not None:
                    sp.wait_ge(x_ready, 1)
                    sp.dma_start(table_out.rearrange("(b p) f -> p b f", p=P), m.x[:, :, 0:D]).then_inc(x_out, 16)
                    sp.wait_ge(x_out, 16)


def relu_pass(nc, m, table_out):
    h_ready, h_out = m.dma_sem("h_ready"), m.dma_sem("h_out")
    with nc.sbuf_tensor("h_keep", [P, BLOCKS, D], F32) as keep, nc.Block() as block:
        @block.vector
        def _(dve):
            nc.vector.tensor_copy(m.x3[:, :, 0:D], m.x[:, :, 0:D])
            nc.vector.tensor_scalar(keep[:, :, :], m.r[:, :, 0:D], 0.0, None, ALU.max).then_inc(h_ready, 1)
            dve.wait_ge(h_ready, 1)
            nc.vector.tensor_copy(m.x[:, :, 0:D], keep[:, :, :]).then_inc(h_ready, 1)

        @block.sync
        def _(sp):
            sp.wait_ge(h_ready, 2)
            sp.dma_start(table_out.rearrange("(b p) f -> p b f", p=P), m.x[:, :, 0:D]).then_inc(h_out, 16)
            sp.wait_ge(h_out, 16)


def degree_pass(nc, m, table3, sums):
    with ExitStack() as ctx:
        sem = ctx.enter_context(stage_semaphores(nc, "degree"))
        step, to_act, from_act = (sem(n) for n in ("step", "to_act", "from_act"))
        out_done = m.dma_sem("degree_out_done")
        t = ctx.enter_context(nc.sbuf_tensor("degree_t", [P, BLOCKS], F32))
        wide_zero = ctx.enter_context(nc.sbuf_tensor("degree_zero", [P, (BLOCKS + 1) * D], F32))
        zero_ready = sem("zero_ready")
        with nc.Block() as block:
            @block.vector
            def _(dve):
                v = nc.vector
                v.memset(wide_zero[:, :], 0.0).then_inc(zero_ready, 1)
                v.tensor_reduce(t[:, :], m.cnt[:, :, :], AX.X, ALU.add).then_inc(step, 1)
                dve.wait_ge(step, 1)
                v.tensor_tensor(t[:, :], t[:, :], m.deg[:, :], ALU.add).then_inc(step, 1)
                dve.wait_ge(step, 2)
                v.tensor_scalar(t[:, :], t[:, :], 1e-5, None, ALU.max).then_inc(to_act, 1)
                dve.wait_ge(from_act, 1)
                v.reciprocal(m.deg[:, :], m.deg[:, :]).then_inc(step, 1)
                dve.wait_ge(step, 3)
                v.tensor_copy(m.x3[:, :, D:D + 1].squeeze(2), m.deg[:, :])
                v.tensor_copy(m.x3[:, :, 0:D], m.x[:, :, 0:D]).then_inc(step, 1)

            @block.scalar
            def _(act):
                act.wait_ge(to_act, 1)
                nc.scalar.activation(m.deg[:, :], t[:, :], ACT.Sqrt).then_inc(from_act, 1)

            @block.sync
            def _(sp):
                sp.wait_ge(zero_ready, 1)
                for s in sums:
                    sp.dma_start(s.rearrange("(p b) f -> p (b f)", p=P), wide_zero[:, :]).then_inc(out_done, 16)
                sp.wait_ge(step, 4)
                sp.dma_start(table3.rearrange("(b p) f -> p b f", p=P), m.x3[:, :, :]).then_inc(out_done, 16)
                sp.wait_ge(out_done, 16 * (len(sums) + 1))


def sheaf_pass(nc, m, table, sums):
    with ExitStack() as ctx:
        sb = lambda n, shape, dt=F32: ctx.enter_context(nc.sbuf_tensor(f"sheaf_{n}", shape, dt))
        pb = lambda n, shape: ctx.enter_context(nc.psum_tensor(f"sheaf_{n}", shape, F32))
        sem = ctx.enter_context(stage_semaphores(nc, "sheaf"))
        idx = sb("idx", [P, 2, G], I32)
        xg = sb("xg", [P, G, X3W])
        xs = sb("xs", [P, G, X3W])
        ends = sb("ends", [P, 2, G])
        node_row = sb("node_row", [P, P])
        sel = sb("sel", [P, G, P])
        sel_t = sb("sel_t", [P, G, P])
        same = sb("same", [P, G, P])
        before = sb("before", [P, G, P])
        repeats = sb("repeats", [P, G])
        to_spare = sb("to_spare", [P, G])
        xs_t = sb("xs_t", [D, G, P])
        hid = sb("hid", [P, G, P])
        v_sb = sb("v_sb", [P, G, 2, D])
        xx = sb("xx", [P, G, 2, D])
        prods = sb("prods", [P, G, 7, D])
        dots = sb("dots", [P, G, 7])
        inv = sb("inv", [P, G, 2])
        q = sb("q", [P, G, 4])
        t2 = sb("t2", [P, G, 2])
        coef = sb("coef", [P, G])
        msg = sb("msg", [P, G, 2, D])
        part = sb("part", [P, G, 2, D])
        out_rows = sb("out_rows", [P, G, D])
        out_idx = sb("out_idx", [P, G], I32)
        nodes = sb("nodes", [P, XW])
        nodes_t = sb("nodes_t", [XW, P])
        node_hid = sb("node_hid", [P, 2 * HID])
        rows_d, rows_s, ps_xs, ps_h = (pb(n, [P, G, P]) for n in ("rows_d", "rows_s", "ps_xs", "ps_h"))
        ps_v = pb("ps_v", [P, G, 64])
        ps_sum = pb("ps_sum", [P, G, D])
        ps_b = pb("ps_b", [P, 2, P])
        acc = pb("acc", [P, D])

        (xs_taken, ends_ready, rows_ready, sel_ready, xs_turned, xs_t_ready, hid_in_psum, hid_ready, v_ready,
         msg_ready, summed, scatter_ready, row_made, block_summed, nodes_ready, nodes_turned, nodes_t_ready,
         node_hid_in_psum, node_hid_ready, sums_taken, step) = (sem(n) for n in (
             "xs_taken", "ends_ready", "rows_ready", "sel_ready", "xs_turned", "xs_t_ready", "hid_in_psum",
             "hid_ready", "v_ready", "msg_ready", "summed", "scatter_ready", "row_made", "block_summed",
             "nodes_ready", "nodes_turned", "nodes_t_ready", "node_hid_in_psum", "node_hid_ready", "sums_taken", "step"))
        idx_in = m.dma_sem("idx_in")
        landed = [m.dma_sem(f"sheaf_landed{k}") for k in range(G)]
        added = [m.dma_sem(f"added{k}") for k in range(G)]
        passed, sp_passed = sem("passed"), sem("sp_passed")

        def block_range(eng, b):
            i0 = eng.value_load(m.steps[0:1, bass.ds(b, 1)], min_val=0, max_val=1 << 20)
            i1 = eng.value_load(m.steps[0:1, bass.ds(b + 1, 1)], min_val=1, max_val=1 << 20)
            return i0, i1

        def step_tiles(eng, b, i, i0, t0):
            return bass.ds(nc.s_assert_within(t0 + (i - i0) * G, 0, TILES - G, skip_runtime_bounds_check_because=BOUNDED), G)

        with nc.Block() as block:
            @block.sync
            def _(sp):
                with sp.Fori(0, BLOCKS) as b:
                    i0, i1 = block_range(sp, b)
                    t0 = sp.value_load(m.tile0[0:1, bass.ds(b, 1)], min_val=0, max_val=REAL_TILES - 1)
                    with sp.Fori(i0, i1) as i:
                        sp.wait_ge(idx_in, i * 16)
                        sp.wait_ge(xs_taken, i)
                        sp.sem_inc(sp_passed, 1)
                        sp.dma_start(idx[:, bass.ds(i & 1, 1), :].squeeze(1),
                                     m.src_i[:, step_tiles(sp, b, i, i0, t0)]).then_inc(idx_in, 16)

            @block.gpsimd
            def _(pool):
                n_less_2 = pool.value_load(m.steps[0:1, BLOCKS + 1:BLOCKS + 2], min_val=2, max_val=1 << 20)

                def gather(i, half):
                    pool.wait_ge(idx_in, (i + 1) * 16)
                    pool.wait_ge(xs_taken, i + 1)
                    pool.sem_inc(passed, 1)
                    for k in range(G):
                        nc.gpsimd.indirect_dma_start(
                            out=xg[:, k, :], out_offset=None, in_=table,
                            in_offset=bass.IndirectOffsetOnAxis(ap=idx[:, half, k:k + 1], axis=0)).then_inc(landed[k], 16)

                def scatter(i):
                    pool.wait_ge(scatter_ready, i + 1)
                    for k in range(G):
                        pool.wait_ge(added[k], i * 16)
                        pool.sem_inc(passed, 1)
                        nc.gpsimd.indirect_dma_start(
                            out=sums[k], out_offset=bass.IndirectOffsetOnAxis(ap=out_idx[:, k:k + 1], axis=0),
                            in_=out_rows[:, k, :], in_offset=None, compute_op=ALU.add).then_inc(added[k], 16)

                gather(0, 0)
                with pool.Fori(0, n_less_2, 2) as i:
                    gather(i + 1, 1)
                    scatter(i)
                    gather(i + 2, 0)
                    scatter(i + 1)
                gather(n_less_2 + 1, 1)
                scatter(n_less_2)
                scatter(n_less_2 + 1)
                for k in range(G):
                    pool.wait_ge(added[k], (n_less_2 + 2) * 16)

            @block.scalar
            def _(act):
                act.sem_inc(xs_taken, 1)
                with act.Fori(0, BLOCKS) as b:
                    i0, i1 = block_range(act, b)
                    t0 = act.value_load(m.tile0[0:1, bass.ds(b, 1)], min_val=0, max_val=REAL_TILES - 1)
                    with act.Fori(i0, i1) as i:
                        tiles = step_tiles(act, b, i, i0, t0)
                        act.wait_ge(scatter_ready, i)
                        nc.scalar.copy(ends[:, 0, :], m.src_i[:, tiles])
                        nc.scalar.copy(ends[:, 1, :], m.dst_f[:, tiles]).then_inc(ends_ready, 1)
                        for k in range(G):
                            act.wait_ge(landed[k], (i + 1) * 16)
                        nc.scalar.copy(xs[:, :, :], xg[:, :, :]).then_inc(xs_taken, 1)
                        act.wait_ge(xs_turned, i + 1)
                        nc.scalar.copy(xs_t[:, :, :], ps_xs[0:D, :, :]).then_inc(xs_t_ready, 1)
                        act.wait_ge(hid_in_psum, i + 1)
                        nc.scalar.activation(hid[:, :, :], ps_h[:, :, :], ACT.Relu).then_inc(hid_ready, 1)

            @block.tensor
            def _(pe):
                mm, tr = nc.tensor.matmul, nc.tensor.transpose
                with pe.Fori(0, BLOCKS) as b:
                    i0, i1 = block_range(pe, b)
                    pe.wait_ge(nodes_ready, b + 1)
                    tr(ps_b[0:XW, 0, :], nodes[:, :], m.ident[:, :]).then_inc(nodes_turned, 1)
                    pe.wait_ge(nodes_t_ready, b + 1)
                    mm(ps_b[:, 1, :], nodes_t[:, :], m.w3n[:, :], start=True, stop=True).then_inc(node_hid_in_psum, 1)
                    pe.wait_ge(node_hid_ready, b + 1)
                    mm(acc[:, :], m.zeros[:, 0:P], m.zeros[:, 0:D], start=True, stop=False, skip_group_check=True)
                    with pe.Fori(i0, i1) as i:
                        pe.wait_ge(ends_ready, i + 1)
                        for k in range(G):
                            tr(rows_d[:, k, :], ends[:, 1, k:k + 1].to_broadcast([P, P]), m.ident[:, :])
                        for k in range(G):
                            last = tr(rows_s[:, k, :], ends[:, 0, k:k + 1].to_broadcast([P, P]), m.ident[:, :])
                        last.then_inc(rows_ready, 1)
                        pe.wait_ge(xs_taken, i + 2)
                        for k in range(G):
                            last = tr(ps_xs[0:D, k, :], xs[:, k, 0:D], m.ident[:, :])
                        last.then_inc(xs_turned, 1)
                        pe.wait_ge(sel_ready, i + 1)
                        mm(ps_h[:, :, :], node_hid[:, :], sel_t[:, :, :], start=True, stop=False)
                        pe.wait_ge(xs_t_ready, i + 1)
                        mm(ps_h[:, :, :], m.w3e[:, :], xs_t[:, :, :], start=False, stop=True).then_inc(hid_in_psum, 1)
                        for k in range(G):
                            mm(ps_v[:, k, 2 * D:3 * D + 1], sel_t[:, k, :], m.x3[:, bass.ds(b, 1), 0:D + 1].squeeze(1),
                               start=True, stop=True)
                        pe.wait_ge(hid_ready, i + 1)
                        for k in range(G):
                            last = mm(ps_v[:, k, 0:2 * D], hid[:, k, :], m.w3v[:, :], start=True, stop=True)
                        last.then_inc(v_ready, 1)
                        pe.wait_ge(msg_ready, i + 1)
                        for k in range(G):
                            last = mm(ps_sum[:, k, :], same[:, k, :], msg[:, k, 1, :], start=True, stop=True)
                        last.then_inc(summed, 1)
                        for k in range(G):
                            last = mm(acc[:, :], sel[:, k, :], msg[:, k, 0, :], start=False, stop=False,
                                      skip_group_check=True)
                        last.then_inc(summed, 1)
                    mm(acc[:, :], m.zeros[:, 0:P], m.zeros[:, 0:D], start=False, stop=True,
                       skip_group_check=True).then_inc(block_summed, 1)
                    pe.wait_ge(sums_taken, b + 1)

            @block.vector
            def _(dve):
                v = nc.vector
                LINKS = 15

                with dve.Fori(0, BLOCKS) as b:
                    i0, i1 = block_range(dve, b)
                    at = bass.ds(b, 1)
                    v.tensor_scalar(node_row[:, :], m.iota[:, :], m.first[:, at], None, ALU.add).then_inc(row_made, 1)
                    v.tensor_copy(nodes[:, :], m.x[:, at, :].squeeze(1)).then_inc(nodes_ready, 1)
                    dve.wait_ge(nodes_turned, b + 1)
                    v.tensor_copy(nodes_t[:, :], ps_b[0:XW, 0, :]).then_inc(nodes_t_ready, 1)
                    dve.wait_ge(node_hid_in_psum, b + 1)
                    v.tensor_copy(node_hid[:, :], ps_b[:, 1, :]).then_inc(node_hid_ready, 1)
                    with dve.Fori(i0, i1) as i:
                        dve.wait_ge(row_made, b + 1)
                        done = [0]

                        def link(ins):
                            done[0] += 1
                            ins.then_inc(step, 1)
                            dve.wait_ge(step, i * LINKS + done[0])

                        dve.wait_ge(rows_ready, i + 1)
                        v.tensor_scalar(sel_t[:, :, :], rows_d[:, :, :], m.node[:, at], None, ALU.is_equal)\
                            .then_inc(sel_ready, 1)
                        for k in range(G):
                            last = v.tensor_scalar(same[:, k, :], rows_s[:, k, :], ends[:, 0, k:k + 1], None, ALU.is_equal)
                        link(last)
                        for k in range(G):
                            v.tensor_scalar(sel[:, k, :], node_row[:, :], ends[:, 1, k:k + 1], None, ALU.is_equal)
                        for k in range(G):
                            last = v.tensor_tensor_reduce(before[:, k, :], same[:, k, :], m.lower[:, :], 1.0, 0.0,
                                                          ALU.mult, ALU.add, accum_out=repeats[:, k:k + 1])
                        link(v.tensor_scalar(to_spare[:, :], ends[:, 0, :], -1.0, m.spare_row[:, 0:1], ALU.mult, ALU.add))
                        link(v.scalar_tensor_tensor(to_spare[:, :], repeats[:, :], 0.0, to_spare[:, :], ALU.is_gt, ALU.mult))
                        dve.wait_ge(v_ready, i + 1)
                        v.tensor_copy(xx[:, :, 0, :], xs[:, :, 0:D])
                        v.tensor_copy(xx[:, :, 1, :], ps_v[:, :, 2 * D:3 * D])
                        v.tensor_tensor(coef[:, :], ps_v[:, :, 3 * D:3 * D + 1].squeeze(2), xs[:, :, D:D + 1].squeeze(2),
                                        ALU.mult)
                        link(v.tensor_tensor(v_sb[:, :, :, :].rearrange("p k n d -> p k (n d)"), ps_v[:, :, 0:2 * D],
                                             m.bias3[:, :].unsqueeze(1).to_broadcast([P, G, 2 * D]), ALU.add))
                        v.tensor_tensor(prods[:, :, 0:2, :], v_sb[:, :, :, :], v_sb[:, :, :, :], ALU.mult)
                        v.tensor_tensor(prods[:, :, 2, :], v_sb[:, :, 0, :], v_sb[:, :, 1, :], ALU.mult)
                        for n in range(2):
                            last = v.tensor_tensor(prods[:, :, 3 + 2 * n:5 + 2 * n, :], v_sb[:, :, :, :],
                                                   xx[:, :, n:n + 1, :].to_broadcast([P, G, 2, D]), ALU.mult)
                        link(last)
                        link(v.tensor_reduce(dots[:, :, :], prods[:, :, :, :], AX.X, ALU.add))
                        link(v.tensor_scalar(inv[:, :, :], dots[:, :, 0:2], 0.5, 0.5e-24, ALU.mult, ALU.max))
                        link(v.reciprocal(inv[:, :, :], inv[:, :, :]))
                        link(v.tensor_tensor(q[:, :, 0:4:3], dots[:, :, 3:7:3], inv[:, :, :], ALU.mult))
                        link(v.tensor_tensor(t2[:, :, :], q[:, :, 0:4:3], dots[:, :, 2:3].to_broadcast([P, G, 2]), ALU.mult))
                        link(v.tensor_tensor(t2[:, :, :], dots[:, :, 4:6], t2[:, :, :], ALU.subtract))
                        link(v.tensor_tensor(q[:, :, 2:0:-1], t2[:, :, :], inv[:, :, ::-1], ALU.mult))
                        v.tensor_tensor(msg[:, :, :, :], v_sb[:, :, 0:1, :].to_broadcast([P, G, 2, D]),
                                        q[:, :, 0:2].unsqueeze(3).to_broadcast([P, G, 2, D]), ALU.mult)
                        link(v.tensor_tensor(part[:, :, :, :], v_sb[:, :, 1:2, :].to_broadcast([P, G, 2, D]),
                                             q[:, :, 2:4].unsqueeze(3).to_broadcast([P, G, 2, D]), ALU.mult))
                        link(v.tensor_tensor(msg[:, :, :, :], msg[:, :, :, :], part[:, :, :, :], ALU.add))
                        link(v.tensor_tensor(part[:, :, :, :], xx[:, :, :, :], msg[:, :, :, :], ALU.subtract))
                        assert done[0] == LINKS, done
                        v.tensor_tensor(msg[:, :, :, :].rearrange("p k n d -> p k (n d)"),
                                        part[:, :, :, :].rearrange("p k n d -> p k (n d)"),
                                        coef[:, :].unsqueeze(2).to_broadcast([P, G, 2 * D]), ALU.mult).then_inc(msg_ready, 1)
                        dve.wait_ge(summed, 2 * i + 2)
                        for k in range(G):
                            dve.wait_ge(added[k], i * 16)
                        v.tensor_tensor(out_idx[:, :], ends[:, 0, :], to_spare[:, :], ALU.add)
                        v.tensor_copy(out_rows[:, :, :], ps_sum[:, :, :]).then_inc(scatter_ready, 1)
                    dve.wait_ge(block_summed, b + 1)
                    v.tensor_copy(m.r[:, at, 0:D].squeeze(1), acc[:, :]).then_inc(sums_taken, 1)


def last_nodes(nc, m, sums, out):
    with ExitStack() as ctx:
        part = [ctx.enter_context(nc.sbuf_tensor(f"part{k}", [P, BLOCKS, D], F32)) for k in range(G)]
        part_in, y_done = m.dma_sem("part_in"), m.dma_sem("y_done")
        with nc.Block() as block:
            @block.sync
            def _(sp):
                for k in range(G):
                    sp.dma_start(part[k][:, :, :], sums[k][0:NODE_PAD, :].rearrange("(b p) f -> p b f", p=P))\
                        .then_inc(part_in, 16)
                sp.wait_ge(part_in, 16 * G)

        def body(v, link, on_act, tmp, one, per_node):
            y, feats = tmp[0][:, :, :], m.x[:, :, 0:D]
            link(v.tensor_tensor(y, m.r[:, :, 0:D], feats, ALU.add))
            for k in range(G):
                link(v.tensor_tensor(y, y, part[k][:, :, :], ALU.add))
            link(v.tensor_scalar(y, y, 0.0, None, ALU.max))
            link(v.tensor_tensor(y, y, feats, ALU.add))

        node_pass(nc, m, "n3", body)
        with nc.Block() as block:
            @block.sync
            def _(sp):
                whole = (BLOCKS - 1) * P
                sp.dma_start(out[0:whole, :].rearrange("(b p) f -> p b f", p=P), m.x[:, 0:BLOCKS - 1, 0:D])\
                    .then_inc(y_done, 16)
                sp.dma_start(out[whole:N_NODES, :], m.x[0:LAST_NODES, BLOCKS - 1, 0:D]).then_inc(y_done, 16)
                sp.wait_ge(y_done, 32)


def gru_nodes(m):
    def body(v, link, on_act, tmp, one, per_node):
        gate = lambda n: m.r[:, :, n * D:(n + 1) * D]
        feats = m.x[:, :, 0:D]
        y = tmp[0][:, :, :]
        on_act(v.tensor_copy(tmp[1][:, :, :], gate(0)), ACT.Sigmoid, tmp[2][:, :, :], tmp[1][:, :, :])
        on_act(v.tensor_copy(tmp[1][:, :, :], gate(1)), ACT.Sigmoid, tmp[3][:, :, :], tmp[1][:, :, :])
        link(v.tensor_tensor(y, tmp[2][:, :, :], gate(3), ALU.mult))
        on_act(v.tensor_tensor(tmp[1][:, :, :], y, gate(2), ALU.add), ACT.Tanh, tmp[2][:, :, :], tmp[1][:, :, :])
        link(v.tensor_tensor(y, feats, tmp[2][:, :, :], ALU.subtract))
        link(v.tensor_tensor(y, y, tmp[3][:, :, :], ALU.mult))
        link(v.tensor_tensor(y, y, tmp[2][:, :, :], ALU.add))
        link(v.tensor_tensor(y, y, feats, ALU.add))
        link(v.tensor_scalar(m.icnt[:, :, :], m.cnt[:, :, :], 1.0, None, ALU.max))
        link(v.reciprocal(m.icnt[:, :, :], m.icnt[:, :, :]))
    return body


def conv_nodes(m):
    def body(v, link, on_act, tmp, one, per_node):
        y, feats = tmp[0][:, :, :], m.x[:, :, 0:D]
        link(v.tensor_tensor(y, m.r[:, :, 0:D], feats, ALU.add))
        link(v.tensor_tensor(y, y, m.bias1[:, :].unsqueeze(1).to_broadcast([P, BLOCKS, D]), ALU.add))
        link(v.tensor_tensor(y, y, feats, ALU.add))
    return body


def relational_nodes(m):
    def body(v, link, on_act, tmp, one, per_node):
        y, z, e = (tmp[n][:, :, :] for n in (0, 1, 2))
        h = m.r[:, :, 0:D]
        link(v.tensor_reduce(one[0][:, :], h, AX.X, ALU.max))
        on_act(v.tensor_tensor(z, h, per_node(one[0]), ALU.subtract), ACT.Exp, e, z)
        on_act(v.tensor_reduce(one[0][:, :], e, AX.X, ALU.add), ACT.Ln, one[1][:, :], one[0][:, :])
        link(v.tensor_tensor(z, z, per_node(one[1]), ALU.subtract))
        link(v.tensor_tensor(y, z, m.x3[:, :, 0:D], ALU.add))
    return body


def gnn_kernel(nc, a, out):
    tables = [nc.dram_tensor(f"table{n}", (NODE_PAD, D), F32, kind="Internal").ap() for n in range(4)]
    table3 = nc.dram_tensor("table_sheaf", (NODE_PAD, X3W), F32, kind="Internal").ap()
    sums = [nc.dram_tensor(f"sums{k}", (NODE_PAD + P, D), F32, kind="Internal").ap() for k in range(G)]
    with ExitStack() as ctx:
        m = memory(nc, ctx)
        load_and_constants(nc, m, a, tables)
        edge_pass(nc, m, "e0", tables[0], count=True, weights=(m.w0a[:, :], m.w0x[:, :]), width=4 * D)
        node_pass(nc, m, "n0", gru_nodes(m), tables[1])
        edge_pass(nc, m, "e1", tables[1], by_attr=a["attr"], weights=(m.w1a[:, :], m.w1b[:, :], m.w1c[:, :]))
        node_pass(nc, m, "n1", conv_nodes(m), tables[2])
        edge_pass(nc, m, "e2", tables[2], by_count=m.icnt, weights=(m.w2a[:, 0, :], m.w2x[:, 0, :]))
        relu_pass(nc, m, tables[3])
        edge_pass(nc, m, "e3", tables[3], by_count=m.icnt, out_degree=True,
                  weights=(m.w2a[:, 1, :], m.w2x[:, 1, :]))
        node_pass(nc, m, "n2", relational_nodes(m))
        degree_pass(nc, m, table3, sums)
        sheaf_pass(nc, m, table3, sums)
        last_nodes(nc, m, sums, out)


def kernel(**inputs):
    import concourse.bacc as bacc
    from concourse.bass_utils import run_bass_kernel_spmd

    names = ("x", "src", "dst", "edge_type_8", "L0_gnn_b_ih", "L0_gnn_b_hh", "L1_gnn_We", "L1_gnn_be", "L1_gnn_bias",
             "L2_gnn_W1", "L2_gnn_root1", "L2_gnn_b1", "L2_gnn_W2", "L2_gnn_root2", "L2_gnn_b2", "L3_gnn_b1", "L3_gnn_b2")
    host = {n: np.ascontiguousarray(inputs[n]) for n in names}
    host["w_ih_t"] = np.ascontiguousarray(np.asarray(inputs["L0_gnn_w_ih"]).T)
    host["w_hh_t"] = np.ascontiguousarray(np.asarray(inputs["L0_gnn_w_hh"]).T)
    emb = np.asarray(inputs["L0_gnn_edge_emb"]).reshape(TYPES, D, D)
    host["emb_t"] = np.ascontiguousarray(emb.transpose(1, 0, 2)).reshape(D, TYPES * D)
    host["w3_1_t"] = np.ascontiguousarray(np.asarray(inputs["L3_gnn_W1"]).T)
    host["w3_2_t"] = np.ascontiguousarray(np.asarray(inputs["L3_gnn_W2"]).T)
    attr = np.asarray(inputs["edge_attr_16"])
    host["attr"] = np.pad(attr, ((0, ATTR_TILES * P - N_EDGES), (0, 0)))

    nc = bacc.Bacc("TRN2", target_bir_lowering=False, num_devices=1)
    arrays, a = {}, {}
    for n, value in host.items():
        arrays[f"in_{n}"] = value
        a[n] = nc.dram_tensor(f"in_{n}", value.shape, mybir.dt.from_np(value.dtype), kind="ExternalInput").ap()
    out = nc.dram_tensor("out_nodes", (N_NODES, D), F32, kind="ExternalOutput").ap()
    gnn_kernel(nc, a, out)
    result = run_bass_kernel_spmd(nc, [arrays], core_ids=[0])
    return result.results[0]["out_nodes"]
```

```python
from contextlib import ExitStack, contextmanager

import concourse.bass as bass
import concourse.mybir as mybir
import numpy as np

F32, I32, BF16 = mybir.dt.float32, mybir.dt.int32, mybir.dt.bfloat16
ALU = mybir.AluOpType
ACT = mybir.ActivationFunctionType
AX = mybir.AxisListType

P = 128
N_NODES = 12500
N_EDGES = 412500
D = 16
TYPES = 8
BLOCKS = -(-N_NODES // P)
NODE_PAD = BLOCKS * P
JUNK = NODE_PAD - 1
LAST_NODES = N_NODES - (BLOCKS - 1) * P
REAL_TILES = -(-N_EDGES // P)
LOAD_GROUPS = -(-REAL_TILES // P)
TILES = LOAD_GROUPS * P
LAST_FULL = N_EDGES // P - (LOAD_GROUPS - 1) * P
LAST_EDGES = N_EDGES % P
RING = 8
G = 4
ATTR_TILES = REAL_TILES + 4 * G
T_BIG = 4096.0
ONES = 2
XW = D + ONES
AW = D + 1
X3W = 20
HID = 64
EPS = 1e-5
BOUNDED = "a block's range ends with the last tile, and a step or two of pads follow"


def memory(nc, ctx):
    m = type("Memory", (), {})()
    m.dma_sem = lambda name: ctx.enter_context(nc.semaphore(name))
    sb = lambda name, shape, dt=F32: ctx.enter_context(nc.sbuf_tensor(name, shape, dt))
    m.src_i = sb("src_i", [P, TILES], I32)
    m.dst_f = sb("dst_f", [P, TILES])
    m.type_b = sb("type_b", [P, TILES], BF16)
    m.src_lo = sb("src_lo", [P, TILES], BF16)
    m.src_hi = sb("src_hi", [P, TILES], BF16)
    m.dst_hi = sb("dst_hi", [P, TILES], BF16)
    m.x = sb("x", [P, BLOCKS, XW])
    m.r = sb("r", [P, BLOCKS, 4 * D])
    m.cnt = sb("cnt", [P, BLOCKS, TYPES])
    m.icnt = sb("icnt", [P, BLOCKS, TYPES])
    m.deg = sb("deg", [P, BLOCKS])
    m.x3 = sb("x3", [P, BLOCKS, X3W])
    m.ident = sb("ident", [P, P])
    m.ident_b = sb("ident_b", [P, P], BF16)
    m.upper = sb("upper", [P, P])
    m.lower = sb("lower", [P, P])
    m.iota = sb("iota", [P, P])
    m.iota_b = sb("iota_b", [P, P], BF16)
    m.iota_blk = sb("iota_blk", [P, BLOCKS])
    m.first = sb("first", [P, BLOCKS])
    m.minus_first = sb("minus_first", [P, BLOCKS])
    m.node = sb("node", [P, BLOCKS])
    m.type_of_col = sb("type_of_col", [P, TYPES * D])
    m.spare_row = sb("spare_row", [P, 1])
    m.zeros = sb("zeros", [P, 384])
    m.steps = sb("steps", [1, BLOCKS + 3], I32)
    m.last = sb("last", [1, BLOCKS], I32)
    m.tile0 = sb("tile0", [1, BLOCKS], I32)
    m.w0a = sb("w0a", [P, 4 * D])
    m.w0x = sb("w0x", [XW, 4 * D])
    m.w1a = sb("w1a", [P, D])
    m.w1b = sb("w1b", [P, D])
    m.w1c = sb("w1c", [D, D])
    m.bias1 = sb("bias1", [P, D])
    m.w2a = sb("w2a", [P, 2, D])
    m.w2x = sb("w2x", [XW, 2, D])
    m.w3n = sb("w3n", [XW, 2 * HID])
    m.w3e = sb("w3e", [D, 2 * HID])
    m.w3v = sb("w3v", [2 * HID, 2 * D])
    m.bias3 = sb("bias3", [P, 2 * D])
    return m


@contextmanager
def stage_semaphores(nc, prefix):
    with ExitStack() as ctx:
        used = []

        def sem(name):
            used.append(ctx.enter_context(nc.semaphore(f"{prefix}_{name}")))
            return used[-1]

        yield sem
        with nc.Block() as block:
            @block.sync
            def _(sp):
                for s in used:
                    sp.sem_clear(s)


def load_and_constants(nc, m, a, tables):
    with ExitStack() as ctx:
        sb = lambda name, shape, dt=F32: ctx.enter_context(nc.sbuf_tensor(name, shape, dt))
        pb = lambda name, shape: ctx.enter_context(nc.psum_tensor(name, shape, F32))
        sem = ctx.enter_context(stage_semaphores(nc, "load"))
        raw = [sb(f"raw{n}", [P, LOAD_GROUPS, P], I32) for n in range(3)]
        row = [sb(f"row{n}", [P, P]) for n in range(3)]
        wih = sb("wih", [D, 3 * D])
        emb = sb("emb", [D, TYPES * D])
        hist_hi = sb("hist_hi", [P, TILES], I32)
        tmin = sb("tmin", [P, LOAD_GROUPS])
        tmax = sb("tmax", [P, LOAD_GROUPS])
        tnum = sb("tnum", [P, LOAD_GROUPS])
        tback = sb("tback", [P, LOAD_GROUPS])
        has = sb("has", [P, BLOCKS, LOAD_GROUPS])
        has2 = sb("has2", [P, BLOCKS, LOAD_GROUPS])
        ends = sb("ends", [P, 2, BLOCKS])
        span = sb("span", [BLOCKS, 6])
        span_i = sb("span_i", [BLOCKS, 2], I32)
        odd = sb("odd", [1, 2], I32)
        ps_w = pb("ps_w", [P, 3 * D])
        ps_t = [pb(f"ps_t{n}", [P, P]) for n in range(3)]
        ps_e = pb("ps_e", [P, 2, P])
        ps_s = pb("ps_s", [1, 2, P])

        ids_in, x_in, w_in, x_out = (m.dma_sem(n) for n in ("ids_in", "x_in", "w_in", "x_out"))
        ids_filled, x_zeroed = sem("ids_filled"), sem("x_zeroed")
        consts_made, zeros_made = sem("consts_made"), sem("zeros_made")
        masks_zeroed = sem("masks_zeroed")
        rows_ready, cols_in_psum, cols_taken, w0_in_psum, ends_ready, ends_in_psum, span_ready, span_in_psum = (
            sem(n) for n in ("rows_ready", "cols_in_psum", "cols_taken", "w0_in_psum", "ends_ready", "ends_in_psum",
                             "span_ready", "span_in_psum"))
        dve_step = sem("dve_step0")
        n_w = [0]

        with nc.Block() as block:
            @block.sync
            def _(sp):
                ids = (a["src"], a["dst"], a["edge_type_8"])
                full = (LOAD_GROUPS - 1) * P * P
                for n in range(3):
                    sp.dma_start(raw[n][:, 0:LOAD_GROUPS - 1, :],
                                 ids[n][0:full].rearrange("(j t e) -> t j e", t=P, e=P)).then_inc(ids_in, 16)
                sp.wait_ge(ids_filled, 3)
                for n in range(3):
                    sp.dma_start(raw[n][0:LAST_FULL, LOAD_GROUPS - 1, :],
                                 ids[n][full:full + LAST_FULL * P].rearrange("(t e) -> t e", e=P)).then_inc(ids_in, 16)
                    sp.dma_start(raw[n][LAST_FULL:LAST_FULL + 1, LOAD_GROUPS - 1, 0:LAST_EDGES],
                                 ids[n][full + LAST_FULL * P:N_EDGES].rearrange("(t e) -> t e", t=1)).then_inc(ids_in, 16)
                sp.wait_ge(x_zeroed, 2)
                whole = (BLOCKS - 1) * P
                sp.dma_start(m.x[:, 0:BLOCKS - 1, 0:D],
                             a["x"][0:whole, :].rearrange("(b p) f -> p b f", p=P)).then_inc(x_in, 16)
                sp.dma_start(m.x[0:LAST_NODES, BLOCKS - 1, 0:D], a["x"][whole:N_NODES, :]).then_inc(x_in, 16)
                sp.wait_ge(x_in, 32)
                sp.dma_start(tables[0].rearrange("(b p) f -> p b f", p=P), m.x[:, :, 0:D]).then_inc(x_out, 16)
                sp.wait_ge(x_out, 16)

            def small_loads():
                row1 = lambda v: v.rearrange("(a j) -> a j", a=1)
                yield wih[:, :], a["w_ih_t"]
                yield emb[:, :], a["emb_t"]
                yield m.w0x[0:D, 0:2 * D], a["w_hh_t"][:, 0:2 * D]
                yield m.w0x[0:D, 3 * D:4 * D], a["w_hh_t"][:, 2 * D:3 * D]
                yield m.w0x[D:D + 1, 0:3 * D], row1(a["L0_gnn_b_ih"])
                yield m.w0x[D + 1:D + 2, 0:2 * D], row1(a["L0_gnn_b_hh"][0:2 * D])
                yield m.w0x[D + 1:D + 2, 3 * D:4 * D], row1(a["L0_gnn_b_hh"][2 * D:3 * D])
                we = a["L1_gnn_We"].rearrange("f (i o) -> (f i) o", o=D)
                yield m.w1a[:, :], we[0:P, :]
                yield m.w1b[:, :], we[P:2 * P, :]
                yield m.w1c[:, :], a["L1_gnn_be"].rearrange("(i o) -> i o", o=D)
                yield m.bias1[:, :], a["L1_gnn_bias"].partition_broadcast(P)
                for layer, (w, root, b) in enumerate((("L2_gnn_W1", "L2_gnn_root1", "L2_gnn_b1"),
                                                      ("L2_gnn_W2", "L2_gnn_root2", "L2_gnn_b2"))):
                    yield m.w2a[:, layer, :], a[w].rearrange("t f o -> (t f) o")
                    yield m.w2x[0:D, layer, :], a[root]
                    yield m.w2x[D:D + 1, layer, :], row1(a[b])
                yield m.w3n[0:D, 0:HID], a["w3_1_t"][D:2 * D, :]
                yield m.w3n[0:D, HID:2 * HID], a["w3_1_t"][0:D, :]
                yield m.w3n[D:D + 1, 0:HID], row1(a["L3_gnn_b1"])
                yield m.w3n[D:D + 1, HID:2 * HID], row1(a["L3_gnn_b1"])
                yield m.w3e[:, 0:HID], a["w3_1_t"][0:D, :]
                yield m.w3e[:, HID:2 * HID], a["w3_1_t"][D:2 * D, :]
                yield m.w3v[0:HID, 0:D], a["w3_2_t"]
                yield m.w3v[HID:2 * HID, D:2 * D], a["w3_2_t"]
                for n in range(2):
                    yield m.bias3[:, n * D:(n + 1) * D], a["L3_gnn_b2"].partition_broadcast(P)

            n_w[0] = len(list(small_loads()))

            @block.scalar
            def _(act):
                act.wait_ge(zeros_made, 4)
                for out, in_ in small_loads():
                    act.dma_start(out, in_).then_inc(w_in, 16)

                def group(j):
                    act.wait_ge(cols_in_psum, j + 1)
                    nc.scalar.copy(m.src_i[:, bass.ds(j * P, P)], ps_t[0][:, :])
                    nc.scalar.copy(m.dst_f[:, bass.ds(j * P, P)], ps_t[1][:, :])
                    nc.scalar.copy(m.type_b[:, bass.ds(j * P, P)], ps_t[2][:, :]).then_inc(cols_taken, 1)

                with act.Fori(0, LOAD_GROUPS) as j:
                    group(j)
                act.wait_ge(w_in, 16 * n_w[0])

            @block.gpsimd
            def _(pool):
                g = nc.gpsimd
                small = dict(allow_small_or_imprecise_dtypes=True)
                g.memset(m.ident[:, :], 0.0).then_inc(masks_zeroed, 1)
                g.memset(m.upper[:, :], 1.0).then_inc(masks_zeroed, 1)
                g.memset(m.lower[:, :], 1.0).then_inc(masks_zeroed, 1)
                pool.wait_ge(masks_zeroed, 3)
                g.affine_select(out=m.ident[:, :], in_=m.ident[:, :], compare_op=ALU.not_equal, fill=1.0, base=0,
                                pattern=[[-1, P]], channel_multiplier=1).then_inc(consts_made, 1)
                g.affine_select(out=m.upper[:, :], in_=m.upper[:, :], compare_op=ALU.is_gt, fill=0.0, base=0,
                                pattern=[[1, P]], channel_multiplier=-1).then_inc(consts_made, 1)
                g.affine_select(out=m.lower[:, :], in_=m.lower[:, :], compare_op=ALU.is_gt, fill=0.0, base=0,
                                pattern=[[-1, P]], channel_multiplier=1).then_inc(consts_made, 1)
                g.iota(m.iota[:, :], [[1, P]], base=0, channel_multiplier=0, **small)
                g.iota(m.iota_b[:, :], [[1, P]], base=0, channel_multiplier=0, **small)
                g.iota(m.iota_blk[:, :], [[1, BLOCKS]], base=0, channel_multiplier=0, **small)
                g.iota(m.first[:, :], [[P, BLOCKS]], base=0, channel_multiplier=0, **small)
                g.iota(m.minus_first[:, :], [[-P, BLOCKS]], base=0, channel_multiplier=0, **small)
                g.iota(m.node[:, :], [[P, BLOCKS]], base=0, channel_multiplier=1, **small)
                g.iota(m.type_of_col[:, :], [[1, TYPES], [0, D]], base=0, channel_multiplier=0, **small)
                g.iota(m.spare_row[:, :], [[0, 1]], base=NODE_PAD, channel_multiplier=1, **small)
                g.iota(tnum[:, :], [[P, LOAD_GROUPS]], base=1, channel_multiplier=1, **small)
                g.iota(tback[:, :], [[-P, LOAD_GROUPS]], base=int(T_BIG), channel_multiplier=-1, **small)\
                    .then_inc(consts_made, 1)

            @block.tensor
            def _(pe):
                pe.wait_ge(consts_made, 4)
                with pe.Fori(0, LOAD_GROUPS) as j:
                    pe.wait_ge(rows_ready, j + 1)
                    pe.wait_ge(cols_taken, j)
                    for n in range(3):
                        last = nc.tensor.transpose(ps_t[n][:, :], row[n][:, :], m.ident[:, :])
                    last.then_inc(cols_in_psum, 1)
                pe.wait_ge(w_in, 16 * n_w[0])
                nc.tensor.matmul(ps_w[:, :], emb[:, :], wih[:, :], start=True, stop=True).then_inc(w0_in_psum, 1)
                pe.wait_ge(ends_ready, 1)
                nc.tensor.transpose(ps_e[0:BLOCKS, 0, :], ends[:, 0, :], m.ident[:, :])
                nc.tensor.transpose(ps_e[0:BLOCKS, 1, :], ends[:, 1, :], m.ident[:, :]).then_inc(ends_in_psum, 1)
                pe.wait_ge(span_ready, 1)
                nc.tensor.matmul(ps_s[0:1, 0, 0:BLOCKS + 1], span[:, 4:5], m.upper[0:BLOCKS, 0:BLOCKS + 1],
                                 start=True, stop=True)
                nc.tensor.matmul(ps_s[0:1, 1, 0:BLOCKS], span[:, 2:3], m.ident[0:BLOCKS, 0:BLOCKS],
                                 start=True, stop=True).then_inc(span_in_psum, 1)

            @block.vector
            def _(dve):
                v = nc.vector
                count = [0]

                def link(ins):
                    count[0] += 1
                    ins.then_inc(dve_step, 1)
                    dve.wait_ge(dve_step, count[0])

                for n, pad in enumerate((JUNK, JUNK, 0)):
                    v.memset(raw[n][:, LOAD_GROUPS - 1, :], pad).then_inc(ids_filled, 1)
                v.memset(m.x[:, :, D:XW], 1.0).then_inc(x_zeroed, 1)
                v.memset(m.x[:, BLOCKS - 1, 0:D], 0.0).then_inc(x_zeroed, 1)
                v.memset(m.w0x[:, :], 0.0).then_inc(zeros_made, 1)
                v.memset(m.w2x[:, :, :], 0.0).then_inc(zeros_made, 1)
                v.memset(m.w3n[:, :], 0.0).then_inc(zeros_made, 1)
                v.memset(m.w3v[:, :], 0.0).then_inc(zeros_made, 1)
                v.memset(m.zeros[:, :], 0.0)
                v.memset(m.x3[:, :, :], 0.0)
                v.memset(m.deg[:, :], 0.0)
                v.memset(m.w0a[:, :], 0.0)
                dve.wait_ge(ids_in, 16 * 9)
                with dve.Fori(0, LOAD_GROUPS) as j:
                    dve.wait_ge(cols_in_psum, j)
                    for n in range(3):
                        last = v.tensor_copy(row[n][:, :], raw[n][:, bass.ds(j, 1), :])
                    last.then_inc(rows_ready, 1)
                v.tensor_reduce(tmin[:, :], raw[1][:, :, :], AX.X, ALU.min)
                link(v.tensor_reduce(tmax[:, :], raw[1][:, :, :], AX.X, ALU.max))
                dve.wait_ge(consts_made, 4)
                v.tensor_copy(m.ident_b[:, :], m.ident[:, :])
                wide = [P, BLOCKS, LOAD_GROUPS]
                per_tile = lambda t: t[:, :].unsqueeze(1).to_broadcast(wide)
                per_block = lambda t: t[:, :].unsqueeze(2).to_broadcast(wide)
                link(v.tensor_scalar(tmin[:, :], tmin[:, :], float(P), None, ALU.subtract))
                v.tensor_tensor(has[:, :, :], per_tile(tmin), per_block(m.first), ALU.is_lt)
                link(v.tensor_tensor(has2[:, :, :], per_tile(tmax), per_block(m.first), ALU.is_ge))
                link(v.tensor_tensor(has[:, :, :], has[:, :, :], has2[:, :, :], ALU.mult))
                link(v.tensor_tensor(has2[:, :, :], has[:, :, :], per_tile(tnum), ALU.mult))
                link(v.tensor_reduce(ends[:, 0, :], has2[:, :, :], AX.X, ALU.max))
                link(v.tensor_tensor(has2[:, :, :], has[:, :, :], per_tile(tback), ALU.mult))
                v.tensor_reduce(ends[:, 1, :], has2[:, :, :], AX.X, ALU.max).then_inc(ends_ready, 1)
                dve.wait_ge(w0_in_psum, 1)
                v.tensor_copy(m.w0a[:, 0:3 * D], ps_w[:, :])
                dve.wait_ge(ends_in_psum, 1)
                link(v.tensor_reduce(span[:, 0:2], ps_e[0:BLOCKS, :, :], AX.X, ALU.max))
                link(v.tensor_scalar(span[:, 2:3], span[:, 1:2], -1.0, T_BIG, ALU.mult, ALU.add))
                link(v.tensor_scalar(span[:, 2:3], span[:, 2:3], float(REAL_TILES - 1), None, ALU.min))
                link(v.tensor_scalar(span[:, 0:1], span[:, 0:1], float(REAL_TILES), None, ALU.min))
                link(v.tensor_tensor(span[:, 3:4], span[:, 0:1], span[:, 2:3], ALU.subtract))
                link(v.tensor_scalar(span_i[:, 0:1], span[:, 3:4], float(G - 1), 1.0, ALU.add, ALU.max))
                link(v.tensor_scalar(span_i[:, 1:2], span_i[:, 0:1], G.bit_length() - 1, None, ALU.arith_shift_right))
                v.tensor_scalar(span[:, 4:5], span_i[:, 1:2], 2.0, None, ALU.max).then_inc(span_ready, 1)
                dve.wait_ge(span_in_psum, 1)
                v.tensor_copy(m.tile0[:, :], ps_s[0:1, 1, 0:BLOCKS])
                link(v.tensor_copy(m.steps[0:1, 0:BLOCKS + 1], ps_s[0:1, 0, 0:BLOCKS + 1]))
                total = m.steps[0:1, BLOCKS:BLOCKS + 1]
                link(v.tensor_scalar(odd[:, 0:1], total, 1, None, ALU.bitwise_and))
                link(v.tensor_tensor(total, total, odd[:, 0:1], ALU.add))
                v.tensor_scalar(m.last[0:1, :], m.steps[0:1, 1:BLOCKS + 1], 1.0, None, ALU.subtract)
                v.tensor_scalar(m.steps[0:1, BLOCKS + 1:BLOCKS + 2], total, 2.0, None, ALU.subtract)
                v.tensor_scalar(m.steps[0:1, BLOCKS + 2:BLOCKS + 3], total, 4.0, None, ALU.subtract)
                dve.wait_ge(cols_taken, LOAD_GROUPS)
                link(v.tensor_scalar(hist_hi[:, :], m.src_i[:, :], P - 1, None, ALU.bitwise_and))
                link(v.tensor_copy(m.src_lo[:, :], hist_hi[:, :]))
                link(v.tensor_scalar(hist_hi[:, :], m.src_i[:, :], 7, None, ALU.logical_shift_right))
                link(v.tensor_copy(m.src_hi[:, :], hist_hi[:, :]))
                link(v.tensor_copy(hist_hi[:, :], m.dst_f[:, :]))
                link(v.tensor_scalar(hist_hi[:, :], hist_hi[:, :], 7, None, ALU.logical_shift_right))
                v.tensor_copy(m.dst_hi[:, :], hist_hi[:, :])


def edge_pass(nc, m, name, table, by_attr=None, count=False, by_count=None, out_degree=(), weights=(), width=D):
    wide = AW if by_attr is not None else TYPES
    cols = wide * D
    turn = RING // G
    with ExitStack() as ctx:
        sb = lambda n, shape, dt=F32: ctx.enter_context(nc.sbuf_tensor(f"{name}_{n}", shape, dt))
        pb = lambda n, shape: ctx.enter_context(nc.psum_tensor(f"{name}_{n}", shape, F32))
        sem = ctx.enter_context(stage_semaphores(nc, name))
        idx = sb("idx", [P, RING], I32)
        xg = sb("xg", [P, RING, D])
        attr = sb("attr", [P, RING, AW]) if by_attr is not None else None
        sel = sb("sel", [P, G, P])
        outer = sb("outer", [P, G, cols + TYPES])
        node_row = sb("node_row", [P, P])
        own = sb("own", [P, cols + XW])
        own_t = sb("own_t", [P, 3, P])
        mask = sb("mask", [P, 2 * G], BF16)
        lo1 = sb("lo1", [P, G, P], BF16)
        hi1 = sb("hi1", [P, G, BLOCKS], BF16)
        zb = sb("zb", [P, P], BF16)
        acc = pb("acc", [P, cols + (TYPES if count else 0)])
        acc_t = pb("acc_t", [P, 3, P])
        res = pb("res", [P, width])
        hist = pb("hist", [P, BLOCKS])
        chunks = []
        for c in range(0, cols, P):
            chunks.append((c, min(P, cols - c)))
        if by_attr is None:
            chunks.append((cols, XW))
        assert len(chunks) == len(weights)

        idx_ready, used, summed = sem("idx_ready"), sem("used"), sem("summed")
        landed = [m.dma_sem(f"{name}_landed{k}") for k in range(G)]
        attr_in = [m.dma_sem(f"{name}_attr_in{k}") for k in range(G)] if by_attr is not None else []
        row_made, block_summed, own_made, own_turned, turned_out, multiplied = (
            sem(n) for n in ("row_made", "block_summed", "own_made", "own_turned", "turned_out", "multiplied"))
        masked, ones_made, passed, sp_passed = sem("masked"), sem("ones_made"), sem("passed"), sem("sp_passed")

        def block_range(eng, b):
            i0 = eng.value_load(m.steps[0:1, bass.ds(b, 1)], min_val=0, max_val=1 << 20)
            i1 = eng.value_load(m.steps[0:1, bass.ds(b + 1, 1)], min_val=1, max_val=1 << 20)
            return i0, i1

        def first_tile(eng, b):
            return eng.value_load(m.tile0[0:1, bass.ds(b, 1)], min_val=0, max_val=REAL_TILES - 1)

        def tile(t0, i, i0, k=0, n=1, tiles=TILES):
            at = nc.s_assert_within(t0 + (i - i0) * G + k, 0, tiles - n, skip_runtime_bounds_check_because=BOUNDED)
            return bass.ds(at, n)

        def slot(i, k):
            return bass.ds((i & (turn - 1)) * G + k, 1)

        with nc.Block() as block:
            @block.scalar
            def _(act):
                def turned(b):
                    act.wait_ge(own_turned, b + 1)
                    for n, (c, w) in enumerate(chunks):
                        last = nc.scalar.copy(own_t[0:w, n, :], acc_t[0:w, n, :])
                    last.then_inc(turned_out, 1)

                def store(b):
                    act.wait_ge(multiplied, b + 1)
                    nc.scalar.copy(m.r[:, bass.ds(b, 1), 0:width].squeeze(1), res[:, :])

                def one_block(b):
                    i0, i1 = block_range(act, b)
                    t0 = first_tile(act, b)
                    with act.Fori(i0, i1) as i:
                        for k in range(G):
                            act.wait_ge(used, i * G + k + 1)
                            nc.scalar.copy(idx[:, slot(i, k)], m.src_i[:, tile(t0, i, i0, k)]).then_inc(idx_ready, 1)

                one_block(0)
                one_block(1)
                turned(0)
                with act.Fori(2, BLOCKS) as b:
                    one_block(b)
                    store(b - 2)
                    turned(b - 1)
                store(BLOCKS - 2)
                turned(BLOCKS - 1)
                store(BLOCKS - 1)

            @block.gpsimd
            def _(pool):
                n_steps = pool.value_load(m.steps[0:1, BLOCKS:BLOCKS + 1], min_val=1, max_val=1 << 20)
                with pool.Fori(0, n_steps, turn) as i:
                    for s in range(turn):
                        for k in range(G):
                            at = s * G + k
                            pool.wait_ge(landed[k], (i + s) * 16)
                            pool.sem_inc(passed, 1)
                            pool.wait_ge(idx_ready, i * G + at + 1)
                            pool.sem_inc(passed, 1)
                            nc.gpsimd.indirect_dma_start(
                                out=xg[:, at, :], out_offset=None, in_=table,
                                in_offset=bass.IndirectOffsetOnAxis(ap=idx[:, at:at + 1], axis=0))\
                                .then_inc(landed[k], 16)

            if by_attr is not None:
                @block.sync
                def _(sp):
                    rows = by_attr.rearrange("(t p) f -> p t f", p=P)
                    with sp.Fori(0, BLOCKS) as b:
                        i0, i1 = block_range(sp, b)
                        t0 = first_tile(sp, b)
                        with sp.Fori(i0, i1) as i:
                            for k in range(G):
                                sp.wait_ge(attr_in[k], i * 16)
                                sp.sem_inc(sp_passed, 1)
                                sp.wait_ge(used, i * G + k + 1)
                                sp.sem_inc(sp_passed, 1)
                                sp.dma_start(attr[:, slot(i, k), 0:D], rows[:, tile(t0, i, i0, k, tiles=ATTR_TILES), :])\
                                    .then_inc(attr_in[k], 16)

            @block.tensor
            def _(pe):
                def multiply(b):
                    pe.wait_ge(turned_out, b + 1)
                    for n, (c, w) in enumerate(chunks):
                        last = nc.tensor.matmul(res[:, :], own_t[0:w, n, :], weights[n], start=n == 0,
                                                stop=n == len(chunks) - 1)
                    last.then_inc(multiplied, 1)

                def one_block(b, before):
                    i0, i1 = block_range(pe, b)
                    zero = m.zeros[:, 0:acc.shape[1]]
                    nc.tensor.matmul(acc[:, :], m.zeros[:, 0:P], zero, start=True, stop=False, skip_group_check=True)
                    with pe.Fori(i0, i1) as i:
                        for k in range(G):
                            pe.wait_ge(used, i * G + k + 1 + RING)
                            if k in out_degree:
                                nc.tensor.matmul(hist[:, :], lo1[:, k, :], hi1[:, k, :], start=False, stop=False,
                                                 skip_group_check=True)
                            nc.tensor.matmul(acc[:, :], sel[:, k, :], outer[:, k, 0:acc.shape[1]], start=False,
                                             stop=False, skip_group_check=True).then_inc(summed, 1)
                    nc.tensor.matmul(acc[:, :], m.zeros[:, 0:P], zero, start=False, stop=True,
                                     skip_group_check=True).then_inc(block_summed, 1)
                    if before:
                        multiply(b - 1)
                    pe.wait_ge(own_made, b + 1)
                    for n, (c, w) in enumerate(chunks):
                        last = nc.tensor.transpose(acc_t[0:w, n, :], own[:, c:c + w], m.ident[:, :])
                    last.then_inc(own_turned, 1)

                if out_degree:
                    pe.wait_ge(ones_made, 1)
                    nc.tensor.matmul(hist[:, :], zb[:, :], zb[:, 0:BLOCKS], start=True, stop=False, skip_group_check=True)
                one_block(0, False)
                with pe.Fori(1, BLOCKS) as b:
                    one_block(b, True)
                multiply(BLOCKS - 1)
                if out_degree:
                    nc.tensor.matmul(hist[:, :], zb[:, :], zb[:, 0:BLOCKS], start=False, stop=True,
                                     skip_group_check=True).then_inc(multiplied, 1)

            @block.vector
            def _(dve):
                v = nc.vector
                if attr is not None:
                    v.memset(attr[:, :, D:AW], 1.0).then_inc(ones_made, 1)
                    dve.wait_ge(ones_made, 1)
                if out_degree:
                    v.memset(zb[:, :], 0.0).then_inc(ones_made, 1)
                dve.sem_inc(used, RING)
                dve.sem_inc(summed, G)
                with dve.Fori(0, BLOCKS) as b:
                    i0, i1 = block_range(dve, b)
                    t0 = first_tile(dve, b)
                    v.tensor_scalar(node_row[:, :], m.iota[:, :], m.first[:, bass.ds(b, 1)], None,
                                    ALU.add).then_inc(row_made, 1)
                    with dve.Fori(i0, i1) as i:
                        dve.wait_ge(row_made, b + 1)
                        if out_degree:
                            dve.wait_ge(summed, i * G + 1)
                            v.tensor_scalar(mask[:, bass.ds((i & 1) * G, G)], m.dst_hi[:, tile(t0, i, i0, 0, G)], m.iota_blk[:, bass.ds(b, 1)],
                                            None, ALU.is_equal).then_inc(masked, 1)
                        for k in range(G):
                            dve.wait_ge(summed, i * G + k + 1)
                            v.tensor_scalar(sel[:, k, :], node_row[:, :], m.dst_f[:, tile(t0, i, i0, k)], None, ALU.is_equal)
                            if k in out_degree:
                                v.tensor_scalar(hi1[:, k, :], m.iota_b[:, 0:BLOCKS], m.src_hi[:, tile(t0, i, i0, k)],
                                                None, ALU.is_equal)
                                dve.wait_ge(masked, i + 1)
                                v.tensor_scalar(lo1[:, k, :], m.iota_b[:, :], m.src_lo[:, tile(t0, i, i0, k)],
                                                mask[:, bass.ds((i & 1) * G + k, 1)], ALU.is_equal, ALU.mult)
                            if count:
                                v.tensor_scalar(outer[:, k, cols:cols + TYPES], m.iota[:, 0:TYPES],
                                                m.type_b[:, tile(t0, i, i0, k)], None, ALU.is_equal)
                            out = outer[:, k, 0:cols].rearrange("p (w f) -> p w f", f=D)
                            feats = xg[:, slot(i, k), :].to_broadcast([P, wide, D])
                            dve.wait_ge(landed[k], (i + 1) * 16)
                            if attr is not None:
                                dve.wait_ge(attr_in[k], (i + 1) * 16)
                                v.tensor_tensor(out, attr[:, slot(i, k), :].squeeze(1).unsqueeze(2).to_broadcast([P, wide, D]),
                                                feats, ALU.mult).then_inc(used, 1)
                            else:
                                kinds = m.type_of_col[:, :].rearrange("p (w f) -> p w f", f=D)
                                v.scalar_tensor_tensor(out, kinds, m.type_b[:, tile(t0, i, i0, k)], feats,
                                                       ALU.is_equal, ALU.mult).then_inc(used, 1)
                    dve.wait_ge(own_turned, b)
                    at = bass.ds(b, 1)
                    v.tensor_copy(own[:, cols:cols + XW], m.x[:, at, :].squeeze(1))
                    dve.wait_ge(block_summed, b + 1)
                    if count:
                        v.tensor_copy(m.cnt[:, at, :].squeeze(1), acc[:, cols:cols + TYPES])
                    if by_count is not None:
                        v.tensor_tensor(own[:, 0:cols].rearrange("p (w f) -> p w f", f=D),
                                        acc[:, 0:cols].rearrange("p (w f) -> p w f", f=D),
                                        by_count[:, at, :].squeeze(1).unsqueeze(2).to_broadcast([P, TYPES, D]),
                                        ALU.mult).then_inc(own_made, 1)
                    else:
                        v.tensor_copy(own[:, 0:cols], acc[:, 0:cols]).then_inc(own_made, 1)
                if out_degree:
                    dve.wait_ge(multiplied, BLOCKS + 1)
                    v.tensor_tensor(m.deg[:, :], m.deg[:, :], hist[:, :], ALU.add)


def node_pass(nc, m, name, body, table_out=None):
    with ExitStack() as ctx:
        sb = lambda n, shape, dt=F32: ctx.enter_context(nc.sbuf_tensor(f"{name}_{n}", shape, dt))
        sem = ctx.enter_context(stage_semaphores(nc, name))
        tmp = [sb(f"tmp{n}", [P, BLOCKS, D]) for n in range(4)]
        one = [sb(f"one{n}", [P, BLOCKS]) for n in range(2)]
        step, to_act, from_act, x_ready = (sem(n) for n in ("step", "to_act", "from_act", "x_ready"))
        x_out = m.dma_sem(f"{name}_x_out")
        asked = []

        with nc.Block() as block:
            @block.vector
            def _(dve):
                v = nc.vector
                count = [0]

                def link(ins):
                    count[0] += 1
                    ins.then_inc(step, 1)
                    dve.wait_ge(step, count[0])

                def on_act(ins, func, out, in_):
                    ins.then_inc(to_act, 1)
                    asked.append((func, out, in_))
                    dve.wait_ge(from_act, len(asked))

                per_node = lambda t: t[:, :].unsqueeze(2).to_broadcast([P, BLOCKS, D])
                body(v, link, on_act, tmp, one, per_node)
                y, z = tmp[0][:, :, :], tmp[1][:, :, :]
                out = m.x[:, :, 0:D]
                link(v.tensor_reduce(one[0][:, :], y, AX.X, ALU.add))
                link(v.tensor_scalar(one[0][:, :], one[0][:, :], 1.0 / D, None, ALU.mult))
                link(v.tensor_tensor(y, y, per_node(one[0]), ALU.subtract))
                link(v.tensor_tensor(z, y, y, ALU.mult))
                link(v.tensor_reduce(one[0][:, :], z, AX.X, ALU.add))
                on_act(v.tensor_scalar(one[0][:, :], one[0][:, :], 1.0 / D, EPS, ALU.mult, ALU.add),
                       ACT.Sqrt, one[1][:, :], one[0][:, :])
                link(v.reciprocal(one[1][:, :], one[1][:, :]))
                v.tensor_tensor(out, y, per_node(one[1]), ALU.mult).then_inc(x_ready, 1)

            @block.scalar
            def _(act):
                for n, (func, out, in_) in enumerate(asked):
                    act.wait_ge(to_act, n + 1)
                    nc.scalar.activation(out, in_, func).then_inc(from_act, 1)

            @block.sync
            def _(sp):
                if table_out is not None:
                    sp.wait_ge(x_ready, 1)
                    sp.dma_start(table_out.rearrange("(b p) f -> p b f", p=P), m.x[:, :, 0:D]).then_inc(x_out, 16)
                    sp.wait_ge(x_out, 16)


def relu_pass(nc, m, table_out):
    h_ready, h_out = m.dma_sem("h_ready"), m.dma_sem("h_out")
    with nc.sbuf_tensor("h_keep", [P, BLOCKS, D], F32) as keep, nc.Block() as block:
        @block.vector
        def _(dve):
            nc.vector.tensor_copy(m.x3[:, :, 0:D], m.x[:, :, 0:D])
            nc.vector.tensor_scalar(keep[:, :, :], m.r[:, :, 0:D], 0.0, None, ALU.max).then_inc(h_ready, 1)
            dve.wait_ge(h_ready, 1)
            nc.vector.tensor_copy(m.x[:, :, 0:D], keep[:, :, :]).then_inc(h_ready, 1)

        @block.sync
        def _(sp):
            sp.wait_ge(h_ready, 2)
            sp.dma_start(table_out.rearrange("(b p) f -> p b f", p=P), m.x[:, :, 0:D]).then_inc(h_out, 16)
            sp.wait_ge(h_out, 16)


def degree_pass(nc, m, table3, sums):
    with ExitStack() as ctx:
        sem = ctx.enter_context(stage_semaphores(nc, "degree"))
        step, to_act, from_act = (sem(n) for n in ("step", "to_act", "from_act"))
        out_done = m.dma_sem("degree_out_done")
        t = ctx.enter_context(nc.sbuf_tensor("degree_t", [P, BLOCKS], F32))
        wide_zero = ctx.enter_context(nc.sbuf_tensor("degree_zero", [P, (BLOCKS + 1) * D], F32))
        zero_ready = sem("zero_ready")
        with nc.Block() as block:
            @block.vector
            def _(dve):
                v = nc.vector
                v.memset(wide_zero[:, :], 0.0).then_inc(zero_ready, 1)
                v.tensor_reduce(t[:, :], m.cnt[:, :, :], AX.X, ALU.add).then_inc(step, 1)
                dve.wait_ge(step, 1)
                v.tensor_tensor(t[:, :], t[:, :], m.deg[:, :], ALU.add).then_inc(step, 1)
                dve.wait_ge(step, 2)
                v.tensor_scalar(t[:, :], t[:, :], 1e-5, None, ALU.max).then_inc(to_act, 1)
                dve.wait_ge(from_act, 1)
                v.reciprocal(m.deg[:, :], m.deg[:, :]).then_inc(step, 1)
                dve.wait_ge(step, 3)
                v.tensor_copy(m.x3[:, :, D:D + 1].squeeze(2), m.deg[:, :])
                v.tensor_copy(m.x3[:, :, 0:D], m.x[:, :, 0:D]).then_inc(step, 1)

            @block.scalar
            def _(act):
                act.wait_ge(to_act, 1)
                nc.scalar.activation(m.deg[:, :], t[:, :], ACT.Sqrt).then_inc(from_act, 1)

            @block.sync
            def _(sp):
                sp.wait_ge(zero_ready, 1)
                for s in sums:
                    sp.dma_start(s.rearrange("(p b) f -> p (b f)", p=P), wide_zero[:, :]).then_inc(out_done, 16)
                sp.wait_ge(step, 4)
                sp.dma_start(table3.rearrange("(b p) f -> p b f", p=P), m.x3[:, :, :]).then_inc(out_done, 16)
                sp.wait_ge(out_done, 16 * (len(sums) + 1))


def sheaf_pass(nc, m, table, sums):
    with ExitStack() as ctx:
        sb = lambda n, shape, dt=F32: ctx.enter_context(nc.sbuf_tensor(f"sheaf_{n}", shape, dt))
        pb = lambda n, shape, dt=F32: ctx.enter_context(nc.psum_tensor(f"sheaf_{n}", shape, dt))
        sem = ctx.enter_context(stage_semaphores(nc, "sheaf"))
        idx = sb("idx", [P, 2, G], I32)
        xg = sb("xg", [P, 2, G, X3W])
        xs = sb("xs", [P, G, X3W])
        dst_ring = sb("dst_ring", [P, 2, G + 1])
        src = sb("src", [P, G])
        dst = sb("dst", [P, G], BF16)
        ends = sb("ends", [P, G])
        sel = sb("sel", [P, G, P], BF16)
        sel_t = sb("sel_t", [P, G, P], BF16)
        same = sb("same", [P, G, P], BF16)
        before = sb("before", [P, G, P], BF16)
        repeats = sb("repeats", [P, G])
        place = sb("place", [P, G])
        xs_t = sb("xs_t", [D, G, P])
        hid = sb("hid", [P, G, P])
        v_sb = sb("v_sb", [P, G, 2, D])
        xx = sb("xx", [P, G, 2, D])
        prods = sb("prods", [P, G, 7, D])
        dots = sb("dots", [P, G, 7])
        inv = sb("inv", [P, G, 2])
        q = sb("q", [P, G, 4])
        t2 = sb("t2", [P, G, 2])
        coef = sb("coef", [P, G])
        msg = sb("msg", [P, G, 2, D])
        part = sb("part", [P, G, 2, D])
        msg3 = sb("msg3", [P, 3, G, 2, D], BF16)
        out_rows = sb("out_rows", [P, G, D])
        out_idx = sb("out_idx", [P, G], I32)
        nodes = sb("nodes", [P, XW])
        nodes_t = sb("nodes_t", [XW, P])
        hid_rest = sb("hid_rest", [P, 2 * HID])
        node_hid3 = sb("node_hid3", [P, 3, 2 * HID], BF16)
        x3_rest = sb("x3_rest", [P, BLOCKS, D + 1])
        x3_3 = sb("x3_3", [P, BLOCKS, 3, D + 1], BF16)
        rows_s, ps_xs, ps_h = (pb(n, [P, G, P]) for n in ("rows_s", "ps_xs", "ps_h"))
        rows_d = pb("rows_d", [P, 2, G, P], BF16)[:, 0, :, :]
        ps_sel = pb("ps_sel", [P, 2, G, P], BF16)[:, 0, :, :]
        ps_v = pb("ps_v", [P, 2, G, 64])[:, 0, :, :]
        shared = pb("shared", [P, 512])
        ps_sum = shared[:, 0:G * D].rearrange("p (k d) -> p k d", d=D)
        ps_b = shared[:, 2 * P:].rearrange("p (n e) -> p n e", e=P)
        acc = pb("acc", [P, 512])[:, 0:3 * D].rearrange("p (n d) -> p n d", d=D)

        (act_passed, src_ready, same_made, x3_split, hid_split, sel_turned, sel_ready, xs_taken, dst_ready, ends_ready, rows_d_ready, rows_s_ready, sel_t_ready, xs_turned, xs_t_ready, hid_in_psum,
         hid_ready, v_ready, v_taken, msg_ready, summed, scatter_ready, block_summed, nodes_ready,
         nodes_turned, nodes_t_ready, node_hid_in_psum, node_hid_ready, sums_taken, step, passed, sp_passed) = (
            sem(n) for n in (
                "act_passed", "src_ready", "same_made", "x3_split", "hid_split", "sel_turned", "sel_ready", "xs_taken", "dst_ready", "ends_ready", "rows_d_ready", "rows_s_ready", "sel_t_ready", "xs_turned",
                "xs_t_ready", "hid_in_psum", "hid_ready", "v_ready", "v_taken", "msg_ready", "summed", "scatter_ready",
                "block_summed", "nodes_ready", "nodes_turned", "nodes_t_ready", "node_hid_in_psum",
                "node_hid_ready", "sums_taken", "step", "passed", "sp_passed"))
        idx_in, dst_in, first_in = (m.dma_sem(n) for n in ("idx_in", "dst_in", "first_in"))
        landed = [m.dma_sem(f"sheaf_landed{k}") for k in range(G)]
        added = [m.dma_sem(f"added{k}") for k in range(G)]

        def first_step(eng, b):
            return eng.value_load(m.steps[0:1, bass.ds(b, 1)], min_val=0, max_val=1 << 20)

        def last_step(eng, b):
            return eng.value_load(m.last[0:1, bass.ds(b, 1)], min_val=0, max_val=1 << 20)

        def first_tile(eng, b):
            return eng.value_load(m.tile0[0:1, bass.ds(b, 1)], min_val=0, max_val=REAL_TILES - 1)

        def step_tiles(t0, steps=0):
            at = nc.s_assert_within(t0 + steps * G, 0, TILES - G, skip_runtime_bounds_check_because=BOUNDED)
            return bass.ds(at, G)

        with nc.Block() as block:
            @block.sync
            def _(sp):
                with sp.Fori(0, BLOCKS) as b:
                    i0, i1 = first_step(sp, b), first_step(sp, b + 1)
                    t0 = first_tile(sp, b)
                    with sp.Fori(i0, i1) as i:
                        sp.wait_ge(idx_in, i * 16)
                        sp.wait_ge(xs_taken, i)
                        sp.sem_inc(sp_passed, 1)
                        sp.dma_start(idx[:, bass.ds(i & 1, 1), :].squeeze(1),
                                     m.src_i[:, step_tiles(t0, i - i0)]).then_inc(idx_in, 16)
                        sp.wait_ge(dst_in, i * 16)
                        sp.sem_inc(sp_passed, 1)
                        sp.dma_start(dst_ring[:, bass.ds(i & 1, 1), 0:G].squeeze(1),
                                     m.dst_f[:, step_tiles(t0, i - i0)]).then_inc(dst_in, 16)
                        sp.wait_ge(first_in, i * 16)
                        sp.sem_inc(sp_passed, 1)
                        sp.dma_start(dst_ring[:, bass.ds(i & 1, 1), G:G + 1].squeeze(1),
                                     m.minus_first[:, bass.ds(b, 1)]).then_inc(first_in, 16)
                n = sp.value_load(m.steps[0:1, BLOCKS:BLOCKS + 1], min_val=2, max_val=1 << 20)
                sp.wait_ge(dst_in, n * 16)
                sp.wait_ge(first_in, n * 16)
                sp.wait_ge(xs_taken, n)
                sp.dma_start(dst_ring[:, 0, 0:G], m.dst_f[:, 0:G]).then_inc(dst_in, 16)
                sp.dma_start(dst_ring[:, 0, G:G + 1], m.minus_first[:, 0:1]).then_inc(first_in, 16)
                sp.wait_ge(dst_in, (n + 1) * 16)
                sp.wait_ge(first_in, (n + 1) * 16)
                sp.sem_inc(sp_passed, 1)

            @block.gpsimd
            def _(pool):
                n_less_4 = pool.value_load(m.steps[0:1, BLOCKS + 2:BLOCKS + 3], min_val=2, max_val=1 << 20)

                def gather(i, half):
                    pool.wait_ge(idx_in, (i + 1) * 16)
                    pool.sem_inc(passed, 1)
                    pool.wait_ge(xs_taken, i)
                    pool.sem_inc(passed, 1)
                    for k in range(G):
                        pool.wait_ge(landed[k], i * 16)
                        pool.sem_inc(passed, 1)
                        nc.gpsimd.indirect_dma_start(
                            out=xg[:, half, k, :], out_offset=None, in_=table,
                            in_offset=bass.IndirectOffsetOnAxis(ap=idx[:, half, k:k + 1], axis=0)).then_inc(landed[k], 16)

                def scatter(i):
                    pool.wait_ge(scatter_ready, i + 1)
                    for k in range(G):
                        pool.wait_ge(added[k], i * 16)
                        pool.sem_inc(passed, 1)
                        nc.gpsimd.indirect_dma_start(
                            out=sums[k], out_offset=bass.IndirectOffsetOnAxis(ap=out_idx[:, k:k + 1], axis=0),
                            in_=out_rows[:, k, :], in_offset=None, compute_op=ALU.add).then_inc(added[k], 16)

                gather(0, 0)
                gather(1, 1)
                gather(2, 0)
                with pool.Fori(0, n_less_4, 2) as i:
                    gather(i + 3, 1)
                    scatter(i)
                    gather(i + 4, 0)
                    scatter(i + 1)
                gather(n_less_4 + 3, 1)
                for k in range(4):
                    scatter(n_less_4 + k)
                for k in range(G):
                    pool.wait_ge(added[k], (n_less_4 + 4) * 16)

            @block.scalar
            def _(act):
                def take_src(i, tiles):
                    act.wait_ge(rows_s_ready, i)
                    act.sem_inc(act_passed, 1)
                    nc.scalar.copy(src[:, :], m.src_i[:, tiles]).then_inc(src_ready, 1)

                def take_dst(i):
                    act.wait_ge(dst_in, (i + 1) * 16)
                    act.wait_ge(first_in, (i + 1) * 16)
                    act.wait_ge(rows_d_ready, i)
                    nc.scalar.activation(dst[:, :], dst_ring[:, bass.ds(i & 1, 1), 0:G].squeeze(1), ACT.Identity,
                                         bias=dst_ring[:, bass.ds(i & 1, 1), G:G + 1].squeeze(1)).then_inc(dst_ready, 1)

                def take_xs(i):
                    act.wait_ge(v_taken, i)
                    for k in range(G):
                        act.wait_ge(landed[k], (i + 1) * 16)
                    nc.scalar.copy(xs[:, :, :], xg[:, bass.ds(i & 1, 1), :, :].squeeze(1)).then_inc(xs_taken, 1)

                def early(i, tiles):
                    take_dst(i + 1)
                    take_src(i, tiles)
                    act.wait_ge(xs_turned, i + 1)
                    nc.scalar.copy(xs_t[:, :, :], ps_xs[0:D, :, :]).then_inc(xs_t_ready, 1)
                    act.wait_ge(hid_in_psum, i + 1)
                    nc.scalar.activation(hid[:, :, :], ps_h[:, :, :], ACT.Relu).then_inc(hid_ready, 1)
                    act.wait_ge(msg_ready, i)
                    act.sem_inc(act_passed, 1)
                    nc.scalar.copy(ends[:, :], m.src_i[:, tiles]).then_inc(ends_ready, 1)

                def late_rows(i):
                    act.wait_ge(summed, 2 * i + 1)
                    for k in range(G):
                        act.wait_ge(added[k], i * 16)
                    nc.scalar.copy(out_idx[:, :], place[:, :])
                    nc.scalar.copy(out_rows[:, :, :], ps_sum[:, :, :]).then_inc(scatter_ready, 1)

                def take_sel(i):
                    act.wait_ge(sel_turned, i + 1)
                    nc.scalar.copy(sel[:, :, :], ps_sel).then_inc(sel_ready, 1)

                def next_sel(i):
                    act.wait_ge(summed, 2 * i + 2)
                    take_sel(i + 1)

                def whole_block(b, end=None):
                    i0, last, t0 = first_step(act, b), last_step(act, b), first_tile(act, b)
                    with act.Fori(i0, end if end is not None else last) as i:
                        early(i + 1, step_tiles(t0, i + 1 - i0))
                        late_rows(i)
                        take_xs(i + 2)
                        next_sel(i)
                    return i0, last, t0

                n_less_2 = act.value_load(m.steps[0:1, BLOCKS + 1:BLOCKS + 2], min_val=2, max_val=1 << 20)
                act.sem_inc(xs_taken, 1)
                take_dst(0)
                take_xs(0)
                early(0, step_tiles(first_tile(act, 0)))
                take_sel(0)
                take_xs(1)
                with act.Fori(0, BLOCKS - 1) as b:
                    _, last, _ = whole_block(b)
                    early(last + 1, step_tiles(first_tile(act, b + 1)))
                    late_rows(last)
                    take_xs(last + 2)
                    next_sel(last)
                i0, last, t0 = whole_block(BLOCKS - 1, n_less_2)
                early(n_less_2 + 1, step_tiles(t0, n_less_2 + 1 - i0))
                late_rows(n_less_2)
                next_sel(n_less_2)
                late_rows(n_less_2 + 1)

            @block.tensor
            def _(pe):
                mm, tr = nc.tensor.matmul, nc.tensor.transpose

                def block_nodes(b):
                    pe.wait_ge(nodes_ready, b + 1)
                    tr(ps_b[0:XW, 0, :], nodes[:, :], m.ident[:, :]).then_inc(nodes_turned, 1)
                    pe.wait_ge(nodes_t_ready, b + 1)
                    mm(ps_b[:, 1, :], nodes_t[:, :], m.w3n[:, :], start=True, stop=True).then_inc(node_hid_in_psum, 1)

                def turn_dst(i):
                    pe.wait_ge(dst_ready, i + 1)
                    pe.wait_ge(sel_t_ready, i)
                    for k in range(G):
                        last = tr(rows_d[:, k, :], dst[:, k:k + 1].to_broadcast([P, P]), m.ident_b[:, :])
                    last.then_inc(rows_d_ready, 1)

                def turn_src(i):
                    pe.wait_ge(src_ready, i + 1)
                    pe.wait_ge(same_made, i)
                    for k in range(G):
                        last = tr(rows_s[:, k, :], src[:, k:k + 1].to_broadcast([P, P]), m.ident[:, :])
                    last.then_inc(rows_s_ready, 1)

                def early(i, b):
                    pe.wait_ge(sel_t_ready, i + 1)
                    for n in range(3):
                        mm(ps_h[:, :, :], node_hid3[:, n, :], sel_t[:, :, :], start=n == 0, stop=False)
                    pe.wait_ge(xs_taken, i + 2)
                    for k in range(G):
                        last = tr(ps_xs[0:D, k, :], xs[:, k, 0:D], m.ident[:, :])
                    last.then_inc(xs_turned, 1)
                    pe.wait_ge(v_taken, i)
                    for k in range(G):
                        for n in range(3):
                            mm(ps_v[:, k, 2 * D:3 * D + 1], sel_t[:, k, :], x3_3[:, bass.ds(b, 1), n, :].squeeze(1),
                               start=n == 0, stop=n == 2)
                    turn_dst(i + 1)
                    pe.wait_ge(xs_t_ready, i + 1)
                    mm(ps_h[:, :, :], m.w3e[:, :], xs_t[:, :, :], start=False, stop=True).then_inc(hid_in_psum, 1)
                    pe.wait_ge(sel_ready, i)
                    for k in range(G):
                        last = tr(ps_sel[:, k, :], sel_t[:, k, :], m.ident_b[:, :])
                    last.then_inc(sel_turned, 1)
                    turn_src(i)
                    pe.wait_ge(hid_ready, i + 1)
                    for k in range(G):
                        last = mm(ps_v[:, k, 0:2 * D], hid[:, k, :], m.w3v[:, :], start=True, stop=True)
                    last.then_inc(v_ready, 1)

                def late_sums(i):
                    pe.wait_ge(scatter_ready, i)
                    pe.wait_ge(msg_ready, i + 1)
                    for k in range(G):
                        for n in range(3):
                            last = mm(ps_sum[:, k, :], same[:, k, :], msg3[:, n, k, 1, :], start=n == 0, stop=n == 2)
                    last.then_inc(summed, 1)
                    pe.wait_ge(sel_ready, i + 1)
                    for k in range(G):
                        last = mm(acc[:, :, :], sel[:, k, :], msg3[:, :, k, 0, :], start=False, stop=False,
                                  skip_group_check=True)
                    last.then_inc(summed, 1)

                def open_block(b):
                    pe.wait_ge(sums_taken, b)
                    mm(acc[:, :, :], m.zeros[:, 0:P], m.zeros[:, 0:3 * D], start=True, stop=False, skip_group_check=True)

                def close_block():
                    mm(acc[:, :, :], m.zeros[:, 0:P], m.zeros[:, 0:3 * D], start=False, stop=True,
                       skip_group_check=True).then_inc(block_summed, 1)

                def whole_block(b):
                    i0, last = first_step(pe, b), last_step(pe, b)
                    open_block(b)
                    with pe.Fori(i0, last) as i:
                        early(i + 1, b)
                        late_sums(i)
                    return last

                block_nodes(0)
                pe.wait_ge(node_hid_ready, 1)
                pe.wait_ge(x3_split, 3)
                turn_dst(0)
                early(0, 0)
                with pe.Fori(0, BLOCKS - 1) as b:
                    last = whole_block(b)
                    pe.wait_ge(scatter_ready, last)
                    block_nodes(b + 1)
                    pe.wait_ge(node_hid_ready, b + 2)
                    early(last + 1, b + 1)
                    late_sums(last)
                    close_block()
                last = whole_block(BLOCKS - 1)
                late_sums(last)
                close_block()

            @block.vector
            def _(dve):
                v = nc.vector
                LINKS = 16

                def block_nodes(b):
                    v.tensor_copy(nodes[:, :], m.x[:, bass.ds(b, 1), :].squeeze(1)).then_inc(nodes_ready, 1)
                    dve.wait_ge(nodes_turned, b + 1)
                    v.tensor_copy(nodes_t[:, :], ps_b[0:XW, 0, :]).then_inc(nodes_t_ready, 1)

                def block_hidden(b):
                    dve.wait_ge(node_hid_in_psum, b + 1)
                    v.tensor_copy(node_hid3[:, 0, :], ps_b[:, 1, :]).then_inc(hid_split, 1)
                    dve.wait_ge(hid_split, 2 * b + 1)
                    v.tensor_tensor(hid_rest[:, :], ps_b[:, 1, :], node_hid3[:, 0, :], ALU.subtract)
                    v.tensor_tensor(node_hid3[:, 1, :], ps_b[:, 1, :], node_hid3[:, 0, :], ALU.subtract)\
                        .then_inc(hid_split, 1)
                    dve.wait_ge(hid_split, 2 * b + 2)
                    v.tensor_tensor(node_hid3[:, 2, :], hid_rest[:, :], node_hid3[:, 1, :], ALU.subtract)\
                        .then_inc(node_hid_ready, 1)

                def select(i):
                    dve.wait_ge(sel_turned, i)
                    dve.wait_ge(rows_d_ready, i + 1)
                    v.tensor_scalar(sel_t[:, :, :], rows_d, m.node[:, 0:1], None, ALU.is_equal)\
                        .then_inc(sel_t_ready, 1)

                def take_v(i):
                    dve.wait_ge(msg_ready, i)
                    dve.wait_ge(v_ready, i + 1)
                    v.tensor_copy(xx[:, :, 0, :], xs[:, :, 0:D])
                    v.tensor_copy(xx[:, :, 1, :], ps_v[:, :, 2 * D:3 * D])
                    v.tensor_tensor(coef[:, :], ps_v[:, :, 3 * D:3 * D + 1].squeeze(2), xs[:, :, D:D + 1].squeeze(2),
                                    ALU.mult)
                    v.tensor_tensor(v_sb[:, :, :, :].rearrange("p k n d -> p k (n d)"), ps_v[:, :, 0:2 * D],
                                    m.bias3[:, :].unsqueeze(1).to_broadcast([P, G, 2 * D]), ALU.add).then_inc(v_taken, 1)

                def late(i):
                    done = [0]

                    def made(ins):
                        done[0] += 1
                        ins.then_inc(step, 1)
                        return done[0]

                    def need(number):
                        dve.wait_ge(step, i * LINKS + number)

                    def link(ins):
                        need(made(ins))

                    dve.wait_ge(summed, 2 * i)
                    dve.wait_ge(ends_ready, i + 1)
                    dve.wait_ge(rows_s_ready, i + 1)
                    v.tensor_tensor(same[:, :, :], rows_s[:, :, :], ends[:, :].unsqueeze(2).to_broadcast([P, G, P]),
                                    ALU.is_equal).then_inc(same_made, 1)
                    dve.wait_ge(v_taken, i + 1)
                    v.tensor_tensor(prods[:, :, 0:2, :], v_sb[:, :, :, :], v_sb[:, :, :, :], ALU.mult)
                    v.tensor_tensor(prods[:, :, 2, :], v_sb[:, :, 0, :], v_sb[:, :, 1, :], ALU.mult)
                    for n in range(2):
                        last = v.tensor_tensor(prods[:, :, 3 + 2 * n:5 + 2 * n, :], v_sb[:, :, :, :],
                                               xx[:, :, n:n + 1, :].to_broadcast([P, G, 2, D]), ALU.mult)
                    prods_made = made(last)
                    dve.wait_ge(same_made, i + 1)
                    for k in range(G):
                        last = v.tensor_tensor_reduce(before[:, k, :], same[:, k, :], m.lower[:, :], 1.0, 0.0,
                                                      ALU.mult, ALU.add, accum_out=repeats[:, k:k + 1])
                    made(last)
                    need(prods_made)
                    dots_made = made(v.tensor_reduce(dots[:, :, :], prods[:, :, :, :], AX.X, ALU.add))
                    dve.wait_ge(scatter_ready, i)
                    place_made = made(v.tensor_scalar(place[:, :], ends[:, :], -1.0, m.spare_row[:, 0:1],
                                                      ALU.mult, ALU.add))
                    need(dots_made)
                    inv_made = made(v.tensor_scalar(inv[:, :, :], dots[:, :, 0:2], 0.5, 0.5e-24, ALU.mult, ALU.max))
                    need(place_made)
                    place_made = made(v.scalar_tensor_tensor(place[:, :], repeats[:, :], 0.0, place[:, :],
                                                             ALU.is_gt, ALU.mult))
                    need(inv_made)
                    inv_made = made(v.reciprocal(inv[:, :, :], inv[:, :, :]))
                    need(place_made)
                    v.tensor_tensor(place[:, :], ends[:, :], place[:, :], ALU.add)
                    need(inv_made)
                    link(v.tensor_tensor(q[:, :, 0:4:3], dots[:, :, 3:7:3], inv[:, :, :], ALU.mult))
                    link(v.tensor_tensor(t2[:, :, :], q[:, :, 0:4:3], dots[:, :, 2:3].to_broadcast([P, G, 2]), ALU.mult))
                    link(v.tensor_tensor(t2[:, :, :], dots[:, :, 4:6], t2[:, :, :], ALU.subtract))
                    link(v.tensor_tensor(q[:, :, 2:0:-1], t2[:, :, :], inv[:, :, ::-1], ALU.mult))
                    v.tensor_tensor(msg[:, :, :, :], v_sb[:, :, 0:1, :].to_broadcast([P, G, 2, D]),
                                    q[:, :, 0:2].unsqueeze(3).to_broadcast([P, G, 2, D]), ALU.mult)
                    link(v.tensor_tensor(part[:, :, :, :], v_sb[:, :, 1:2, :].to_broadcast([P, G, 2, D]),
                                         q[:, :, 2:4].unsqueeze(3).to_broadcast([P, G, 2, D]), ALU.mult))
                    link(v.tensor_tensor(msg[:, :, :, :], msg[:, :, :, :], part[:, :, :, :], ALU.add))
                    link(v.tensor_tensor(part[:, :, :, :], xx[:, :, :, :], msg[:, :, :, :], ALU.subtract))
                    flat = lambda t: t.rearrange("p k n d -> p k (n d)")
                    by_coef = coef[:, :].unsqueeze(2).to_broadcast([P, G, 2 * D])
                    v.tensor_tensor(flat(msg3[:, 0, :, :, :]), flat(part[:, :, :, :]), by_coef, ALU.mult)
                    link(v.tensor_tensor(flat(msg[:, :, :, :]), flat(part[:, :, :, :]), by_coef, ALU.mult))
                    v.tensor_tensor(msg3[:, 1, :, :, :], msg[:, :, :, :], msg3[:, 0, :, :, :], ALU.subtract)
                    link(v.tensor_tensor(part[:, :, :, :], msg[:, :, :, :], msg3[:, 0, :, :, :], ALU.subtract))
                    assert done[0] == LINKS, done
                    v.tensor_tensor(msg3[:, 2, :, :, :], part[:, :, :, :], msg3[:, 1, :, :, :], ALU.subtract)\
                        .then_inc(msg_ready, 1)

                def whole_block(b):
                    i0, last = first_step(dve, b), last_step(dve, b)
                    with dve.Fori(i0, last) as i:
                        take_v(i)
                        late(i)
                        select(i + 2)
                    return last

                def take_sums(b):
                    dve.wait_ge(block_summed, b + 1)
                    v.tensor_reduce(m.r[:, bass.ds(b, 1), 0:D].squeeze(1), acc[:, :, :].rearrange("p n d -> p d n"),
                                    AX.X, ALU.add).then_inc(sums_taken, 1)

                v.tensor_copy(x3_3[:, :, 0, :], m.x3[:, :, 0:D + 1]).then_inc(x3_split, 1)
                dve.wait_ge(x3_split, 1)
                v.tensor_tensor(x3_rest[:, :, :], m.x3[:, :, 0:D + 1], x3_3[:, :, 0, :], ALU.subtract)
                v.tensor_tensor(x3_3[:, :, 1, :], m.x3[:, :, 0:D + 1], x3_3[:, :, 0, :], ALU.subtract)\
                    .then_inc(x3_split, 1)
                dve.wait_ge(x3_split, 2)
                v.tensor_tensor(x3_3[:, :, 2, :], x3_rest[:, :, :], x3_3[:, :, 1, :], ALU.subtract)\
                    .then_inc(x3_split, 1)
                block_nodes(0)
                block_hidden(0)
                select(0)
                select(1)
                with dve.Fori(0, BLOCKS - 1) as b:
                    last = whole_block(b)
                    block_nodes(b + 1)
                    take_v(last)
                    block_hidden(b + 1)
                    late(last)
                    select(last + 2)
                    take_sums(b)
                last = whole_block(BLOCKS - 1)
                take_v(last)
                late(last)
                take_sums(BLOCKS - 1)


def last_nodes(nc, m, sums, out):
    with ExitStack() as ctx:
        part = [ctx.enter_context(nc.sbuf_tensor(f"part{k}", [P, BLOCKS, D], F32)) for k in range(G)]
        part_in, y_done = m.dma_sem("part_in"), m.dma_sem("y_done")
        with nc.Block() as block:
            @block.sync
            def _(sp):
                for k in range(G):
                    sp.dma_start(part[k][:, :, :], sums[k][0:NODE_PAD, :].rearrange("(b p) f -> p b f", p=P))\
                        .then_inc(part_in, 16)
                sp.wait_ge(part_in, 16 * G)

        def body(v, link, on_act, tmp, one, per_node):
            y, feats = tmp[0][:, :, :], m.x[:, :, 0:D]
            link(v.tensor_tensor(y, m.r[:, :, 0:D], feats, ALU.add))
            for k in range(G):
                link(v.tensor_tensor(y, y, part[k][:, :, :], ALU.add))
            link(v.tensor_scalar(y, y, 0.0, None, ALU.max))
            link(v.tensor_tensor(y, y, feats, ALU.add))

        node_pass(nc, m, "n3", body)
        with nc.Block() as block:
            @block.sync
            def _(sp):
                whole = (BLOCKS - 1) * P
                sp.dma_start(out[0:whole, :].rearrange("(b p) f -> p b f", p=P), m.x[:, 0:BLOCKS - 1, 0:D])\
                    .then_inc(y_done, 16)
                sp.dma_start(out[whole:N_NODES, :], m.x[0:LAST_NODES, BLOCKS - 1, 0:D]).then_inc(y_done, 16)
                sp.wait_ge(y_done, 32)


def gru_nodes(m):
    def body(v, link, on_act, tmp, one, per_node):
        gate = lambda n: m.r[:, :, n * D:(n + 1) * D]
        feats = m.x[:, :, 0:D]
        y = tmp[0][:, :, :]
        on_act(v.tensor_copy(tmp[1][:, :, :], gate(0)), ACT.Sigmoid, tmp[2][:, :, :], tmp[1][:, :, :])
        on_act(v.tensor_copy(tmp[1][:, :, :], gate(1)), ACT.Sigmoid, tmp[3][:, :, :], tmp[1][:, :, :])
        link(v.tensor_tensor(y, tmp[2][:, :, :], gate(3), ALU.mult))
        on_act(v.tensor_tensor(tmp[1][:, :, :], y, gate(2), ALU.add), ACT.Tanh, tmp[2][:, :, :], tmp[1][:, :, :])
        link(v.tensor_tensor(y, feats, tmp[2][:, :, :], ALU.subtract))
        link(v.tensor_tensor(y, y, tmp[3][:, :, :], ALU.mult))
        link(v.tensor_tensor(y, y, tmp[2][:, :, :], ALU.add))
        link(v.tensor_tensor(y, y, feats, ALU.add))
        link(v.tensor_scalar(m.icnt[:, :, :], m.cnt[:, :, :], 1.0, None, ALU.max))
        link(v.reciprocal(m.icnt[:, :, :], m.icnt[:, :, :]))
    return body


def conv_nodes(m):
    def body(v, link, on_act, tmp, one, per_node):
        y, feats = tmp[0][:, :, :], m.x[:, :, 0:D]
        link(v.tensor_tensor(y, m.r[:, :, 0:D], feats, ALU.add))
        link(v.tensor_tensor(y, y, m.bias1[:, :].unsqueeze(1).to_broadcast([P, BLOCKS, D]), ALU.add))
        link(v.tensor_tensor(y, y, feats, ALU.add))
    return body


def relational_nodes(m):
    def body(v, link, on_act, tmp, one, per_node):
        y, z, e = (tmp[n][:, :, :] for n in (0, 1, 2))
        h = m.r[:, :, 0:D]
        link(v.tensor_reduce(one[0][:, :], h, AX.X, ALU.max))
        on_act(v.tensor_tensor(z, h, per_node(one[0]), ALU.subtract), ACT.Exp, e, z)
        on_act(v.tensor_reduce(one[0][:, :], e, AX.X, ALU.add), ACT.Ln, one[1][:, :], one[0][:, :])
        link(v.tensor_tensor(z, z, per_node(one[1]), ALU.subtract))
        link(v.tensor_tensor(y, z, m.x3[:, :, 0:D], ALU.add))
    return body


def gnn_kernel(nc, a, out):
    tables = [nc.dram_tensor(f"table{n}", (NODE_PAD, D), F32, kind="Internal").ap() for n in range(4)]
    table3 = nc.dram_tensor("table_sheaf", (NODE_PAD, X3W), F32, kind="Internal").ap()
    sums = [nc.dram_tensor(f"sums{k}", (NODE_PAD + P, D), F32, kind="Internal").ap() for k in range(G)]
    with ExitStack() as ctx:
        m = memory(nc, ctx)
        load_and_constants(nc, m, a, tables)
        edge_pass(nc, m, "e0", tables[0], count=True, weights=(m.w0a[:, :], m.w0x[:, :]), width=4 * D)
        node_pass(nc, m, "n0", gru_nodes(m), tables[1])
        edge_pass(nc, m, "e1", tables[1], by_attr=a["attr"], weights=(m.w1a[:, :], m.w1b[:, :], m.w1c[:, :]))
        node_pass(nc, m, "n1", conv_nodes(m), tables[2])
        edge_pass(nc, m, "e2", tables[2], by_count=m.icnt, out_degree=range(0, G // 2),
                  weights=(m.w2a[:, 0, :], m.w2x[:, 0, :]))
        relu_pass(nc, m, tables[3])
        edge_pass(nc, m, "e3", tables[3], by_count=m.icnt, out_degree=range(G // 2, G),
                  weights=(m.w2a[:, 1, :], m.w2x[:, 1, :]))
        node_pass(nc, m, "n2", relational_nodes(m))
        degree_pass(nc, m, table3, sums)
        sheaf_pass(nc, m, table3, sums)
        last_nodes(nc, m, sums, out)


def kernel(**inputs):
    import concourse.bacc as bacc
    from concourse.bass_utils import run_bass_kernel_spmd

    names = ("x", "src", "dst", "edge_type_8", "L0_gnn_b_ih", "L0_gnn_b_hh", "L1_gnn_We", "L1_gnn_be", "L1_gnn_bias",
             "L2_gnn_W1", "L2_gnn_root1", "L2_gnn_b1", "L2_gnn_W2", "L2_gnn_root2", "L2_gnn_b2", "L3_gnn_b1", "L3_gnn_b2")
    host = {n: np.ascontiguousarray(inputs[n]) for n in names}
    host["w_ih_t"] = np.ascontiguousarray(np.asarray(inputs["L0_gnn_w_ih"]).T)
    host["w_hh_t"] = np.ascontiguousarray(np.asarray(inputs["L0_gnn_w_hh"]).T)
    emb = np.asarray(inputs["L0_gnn_edge_emb"]).reshape(TYPES, D, D)
    host["emb_t"] = np.ascontiguousarray(emb.transpose(1, 0, 2)).reshape(D, TYPES * D)
    host["w3_1_t"] = np.ascontiguousarray(np.asarray(inputs["L3_gnn_W1"]).T)
    host["w3_2_t"] = np.ascontiguousarray(np.asarray(inputs["L3_gnn_W2"]).T)
    attr = np.asarray(inputs["edge_attr_16"])
    host["attr"] = np.pad(attr, ((0, ATTR_TILES * P - N_EDGES), (0, 0)))

    nc = bacc.Bacc("TRN2", target_bir_lowering=False, num_devices=1)
    arrays, a = {}, {}
    for n, value in host.items():
        arrays[f"in_{n}"] = value
        a[n] = nc.dram_tensor(f"in_{n}", value.shape, mybir.dt.from_np(value.dtype), kind="ExternalInput").ap()
    out = nc.dram_tensor("out_nodes", (N_NODES, D), F32, kind="ExternalOutput").ap()
    gnn_kernel(nc, a, out)
    result = run_bass_kernel_spmd(nc, [arrays], core_ids=[0])
    return result.results[0]["out_nodes"]
```
